# Optimizing a Trainium2 kernel written in Bass

```python
import numpy as np
import jax
import jax.numpy as jnp

def _softmax(x, axis=-1):
    return jax.nn.softmax(x, axis=axis)

def _gelu(x):
    return jax.nn.gelu(x, approximate=True)

def _silu(x):
    return jax.nn.silu(x)

def _sigmoid(x):
    return jax.nn.sigmoid(x)

def _layernorm(x, axis=-1, eps=1e-05):
    m = jnp.mean(x, axis=axis, keepdims=True)
    v = jnp.var(x, axis=axis, keepdims=True)
    return (x - m) / jnp.sqrt(v + eps)

def _scatter_add(tgt, idx, src, axis=0):
    return tgt.at[idx].add(src)

def _segment_sum(src, seg, n):
    return jax.ops.segment_sum(src, seg, n)
kernel_name = 'mk_seq_postln_d1_jaxref_r4_009b3a'

def setup_inputs(seed: int=0):
    np.random.seed(seed)
    _w = jnp.asarray

    def _L0_attn_setup():
        import jax, jax.numpy as jnp
        import numpy as np
        D_MODEL = 256
        EXPAND = 2
        D_INNER = D_MODEL * EXPAND
        D_STATE = 16
        FFN_HIDDEN = (D_MODEL * 4 * 2 // 3 + 63) // 64 * 64
        EPS = 1e-06

        def rmsnorm(x, w):
            return x * jax.lax.rsqrt(jnp.mean(x * x, axis=-1, keepdims=True) + EPS) * w

        def selective_scan(z, dt_w, dt_b, x_proj_w, A_log, Dp):
            dt = jax.nn.softplus(jnp.einsum('bld,ed->ble', z, dt_w) + dt_b)
            BC = jnp.einsum('bld,nd->bln', z, x_proj_w)
            Bm, Cm = (BC[..., :D_STATE], BC[..., D_STATE:])
            A = -jnp.exp(A_log)
            dA = jnp.exp(dt[..., None] * A)
            dBz = (dt * z)[..., None] * Bm[:, :, None, :]

            def combine(e1, e2):
                a1, b1 = e1
                a2, b2 = e2
                return (a1 * a2, a2 * b1 + b2)
            _, h = jax.lax.associative_scan(combine, (dA, dBz), axis=1)
            y = jnp.einsum('bldn,bln->bld', h, Cm) + z * Dp
            return y
        key = jax.random.key(seed)
        ks = jax.random.split(key, 12)
        s = 0.02
        inp = {'x': jax.random.normal(ks[0], (2, 256, D_MODEL), dtype=jnp.float32), 'norm1_w': jnp.ones((D_MODEL,), jnp.float32), 'in_proj_w': jax.random.normal(ks[1], (D_INNER, D_MODEL), jnp.float32) * s, 'gate_proj_w': jax.random.normal(ks[2], (D_INNER, D_MODEL), jnp.float32) * s, 'dt_w': jax.random.normal(ks[3], (D_INNER, D_INNER), jnp.float32) * s, 'dt_b': jnp.full((D_INNER,), -2.0, jnp.float32), 'x_proj_w': jax.random.normal(ks[4], (2 * D_STATE, D_INNER), jnp.float32) * s, 'A_log': jnp.broadcast_to(jnp.log(jnp.arange(1, D_STATE + 1, dtype=jnp.float32)), (D_INNER, D_STATE)).copy(), 'Dp': jnp.ones((D_INNER,), jnp.float32), 'out_proj_w': jax.random.normal(ks[5], (D_MODEL, D_INNER), jnp.float32) * s, 'ffn_norm_w': jnp.ones((D_MODEL,), jnp.float32), 'ffn_gate_w': jax.random.normal(ks[6], (FFN_HIDDEN, D_MODEL), jnp.float32) * s, 'ffn_up_w': jax.random.normal(ks[7], (FFN_HIDDEN, D_MODEL), jnp.float32) * s, 'ffn_down_w': jax.random.normal(ks[8], (D_MODEL, FFN_HIDDEN), jnp.float32) * s}
        return inp
    _L0_attn_in = _L0_attn_setup()

    def _L0_ffn_setup():
        import jax, jax.numpy as jnp
        import numpy as np
        key = jax.random.key(seed)
        ks = jax.random.split(key, 5)
        B, Sq, M, E, H = (4, 512, 256, 8, 1024)
        x = jax.random.normal(ks[0], (B, Sq, M), dtype=jnp.float32)
        wg = jax.random.normal(ks[1], (M, E), dtype=jnp.float32) * (1.0 / np.sqrt(M))
        w1 = jax.random.normal(ks[2], (E, M, H), dtype=jnp.float32) * (1.0 / np.sqrt(M))
        b1 = jnp.zeros((E, H), dtype=jnp.float32)
        w2 = jax.random.normal(ks[3], (E, H, M), dtype=jnp.float32) * (1.0 / np.sqrt(H))
        b2 = jnp.zeros((E, M), dtype=jnp.float32)
        return {'x': x, 'wg': wg, 'w1': w1, 'b1': b1, 'w2': w2, 'b2': b2}
    _L0_ffn_in = _L0_ffn_setup()
    _d = {'L0_attn_x': _L0_attn_in['x'], 'L0_attn_norm1_w': _L0_attn_in['norm1_w'], 'L0_attn_in_proj_w': _L0_attn_in['in_proj_w'], 'L0_attn_gate_proj_w': _L0_attn_in['gate_proj_w'], 'L0_attn_dt_w': _L0_attn_in['dt_w'], 'L0_attn_dt_b': _L0_attn_in['dt_b'], 'L0_attn_x_proj_w': _L0_attn_in['x_proj_w'], 'L0_attn_A_log': _L0_attn_in['A_log'], 'L0_attn_Dp': _L0_attn_in['Dp'], 'L0_attn_out_proj_w': _L0_attn_in['out_proj_w'], 'L0_attn_ffn_norm_w': _L0_attn_in['ffn_norm_w'], 'L0_attn_ffn_gate_w': _L0_attn_in['ffn_gate_w'], 'L0_attn_ffn_up_w': _L0_attn_in['ffn_up_w'], 'L0_attn_ffn_down_w': _L0_attn_in['ffn_down_w'], 'L0_ffn_wg': _L0_ffn_in['wg'], 'L0_ffn_w1': _L0_ffn_in['w1'], 'L0_ffn_b1': _L0_ffn_in['b1'], 'L0_ffn_w2': _L0_ffn_in['w2'], 'L0_ffn_b2': _L0_ffn_in['b2']}
    _x0 = _d['L0_attn_x']
    _d['L0_attn_x'] = jax.random.normal(jax.random.fold_in(jax.random.key(seed), 1), (4, 2048, 256), dtype=_x0.dtype)
    del _x0
    return _d

def reference(L0_attn_x, L0_attn_norm1_w, L0_attn_in_proj_w, L0_attn_gate_proj_w, L0_attn_dt_w, L0_attn_dt_b, L0_attn_x_proj_w, L0_attn_A_log, L0_attn_Dp, L0_attn_out_proj_w, L0_attn_ffn_norm_w, L0_attn_ffn_gate_w, L0_attn_ffn_up_w, L0_attn_ffn_down_w, L0_ffn_wg, L0_ffn_w1, L0_ffn_b1, L0_ffn_w2, L0_ffn_b2):

    def _L0_attn_ref(x, norm1_w, in_proj_w, gate_proj_w, dt_w, dt_b, x_proj_w, A_log, Dp, out_proj_w, ffn_norm_w, ffn_gate_w, ffn_up_w, ffn_down_w):
        import jax, jax.numpy as jnp
        import numpy as np
        D_MODEL = 256
        EXPAND = 2
        D_INNER = D_MODEL * EXPAND
        D_STATE = 16
        FFN_HIDDEN = (D_MODEL * 4 * 2 // 3 + 63) // 64 * 64
        EPS = 1e-06

        def rmsnorm(x, w):
            return x * jax.lax.rsqrt(jnp.mean(x * x, axis=-1, keepdims=True) + EPS) * w

        def selective_scan(z, dt_w, dt_b, x_proj_w, A_log, Dp):
            dt = jax.nn.softplus(jnp.einsum('bld,ed->ble', z, dt_w) + dt_b)
            BC = jnp.einsum('bld,nd->bln', z, x_proj_w)
            Bm, Cm = (BC[..., :D_STATE], BC[..., D_STATE:])
            A = -jnp.exp(A_log)
            dA = jnp.exp(dt[..., None] * A)
            dBz = (dt * z)[..., None] * Bm[:, :, None, :]

            def combine(e1, e2):
                a1, b1 = e1
                a2, b2 = e2
                return (a1 * a2, a2 * b1 + b2)
            _, h = jax.lax.associative_scan(combine, (dA, dBz), axis=1)
            y = jnp.einsum('bldn,bln->bld', h, Cm) + z * Dp
            return y
        residual = x
        h = rmsnorm(x, norm1_w)
        z = jnp.einsum('bld,ed->ble', h, in_proj_w)
        gate = jax.nn.sigmoid(jnp.einsum('bld,ed->ble', h, gate_proj_w))
        z = z * gate
        ssm_out = selective_scan(z, dt_w, dt_b, x_proj_w, A_log, Dp)
        x = residual + jnp.einsum('ble,de->bld', ssm_out, out_proj_w)
        hn = rmsnorm(x, ffn_norm_w)
        ff = jnp.einsum('blh,dh->bld', jax.nn.silu(jnp.einsum('bld,hd->blh', hn, ffn_gate_w)) * jnp.einsum('bld,hd->blh', hn, ffn_up_w), ffn_down_w)
        return x + ff

    def _L0_ffn_ref(x, wg, w1, b1, w2, b2):
        import jax, jax.numpy as jnp
        import numpy as np
        B, Sq, M = x.shape
        E = wg.shape[1]
        S = B * Sq
        C = S // E
        xt = x.reshape(S, M)
        gates = jax.nn.softmax(xt @ wg, axis=-1)
        expert_idx = jnp.argmax(gates, axis=-1)
        mask1 = jax.nn.one_hot(expert_idx, E, dtype=xt.dtype)
        locations = jnp.cumsum(mask1, axis=0) - 1.0
        pos = jnp.sum(locations * mask1, axis=1).astype(jnp.int32)
        keep = (pos < C).astype(xt.dtype)
        gate_val = jnp.sum(gates * mask1, axis=1) * keep
        slot = expert_idx.astype(jnp.int32) * C + jnp.clip(pos, 0, C - 1)
        disp = jnp.zeros((E * C, M), dtype=xt.dtype).at[slot].add(xt * keep[:, None])
        disp = disp.reshape(E, C, M)
        h = jax.nn.relu(jnp.einsum('ecm,emh->ech', disp, w1) + b1[:, None, :])
        eo = jnp.einsum('ech,ehm->ecm', h, w2) + b2[:, None, :]
        out = eo.reshape(E * C, M)[slot] * gate_val[:, None]
        return out.reshape(B, Sq, M)
    x = L0_attn_x
    x = _layernorm(x + _L0_attn_ref(x, L0_attn_norm1_w, L0_attn_in_proj_w, L0_attn_gate_proj_w, L0_attn_dt_w, L0_attn_dt_b, L0_attn_x_proj_w, L0_attn_A_log, L0_attn_Dp, L0_attn_out_proj_w, L0_attn_ffn_norm_w, L0_attn_ffn_gate_w, L0_attn_ffn_up_w, L0_attn_ffn_down_w), axis=-1)
    x = _layernorm(x + _L0_ffn_ref(x, L0_ffn_wg, L0_ffn_w1, L0_ffn_b1, L0_ffn_w2, L0_ffn_b2), axis=-1)
    return x

_drawn_inputs = setup_inputs


def setup_inputs(seed=0):
    import zlib

    import numpy as np

    out = dict(_drawn_inputs(seed))
    spreads = {'L0_attn_norm1_w': (1.0, 0.6),
     'L0_attn_dt_b': (-2.0, 0.6),
     'L0_attn_Dp': (1.0, 0.6),
     'L0_attn_ffn_norm_w': (1.0, 0.6),
     'L0_ffn_b1': (0.0, 0.302),
     'L0_ffn_b2': (0.0, 0.1)}
    factors = {'L0_attn_gate_proj_w': 3.285,
     'L0_attn_dt_w': 8.0,
     'L0_attn_x_proj_w': 8.0,
     'L0_attn_A_log': 8.0}
    for name, (base, spread) in spreads.items():
        noise = np.random.default_rng([zlib.crc32(name.encode()), seed]).standard_normal(out[name].shape)
        drawn = base * np.exp(spread * noise) if base else spread * noise
        out[name] = jnp.asarray(drawn.astype(out[name].dtype))
    for name, factor in factors.items():
        out[name] = (out[name] * factor).astype(out[name].dtype)
    return out
```

```python
from contextlib import ExitStack

import concourse.bass as bass
from concourse import mybir
from concourse.alu_op_type import AluOpType as ALU

F32 = mybir.dt.float32
BF16 = mybir.dt.bfloat16
U32 = mybir.dt.uint32
ACT = mybir.ActivationFunctionType
AX = mybir.AxisListType

P = 128
T = 512
NT = T // P
ROW = 260
RMS_EPS = 1e-6
LN_EPS = 1e-5
EXP_CAP = 1e18
NOWHERE = 65536.0
EXP_LN = "natural_log_exp_and_others"


def some(count):
    return not isinstance(count, int) or count > 0


def first(count, start):
    return isinstance(count, int) and count == start


def constants_layout(D, NE, NCH):
    at, o = {}, 0
    for name, n in (("ident", P), ("earlier", P), ("ones", P), ("rank", NE), ("base", NE), ("keep", NCH + 1), ("token", NT)):
        at[name] = (o, o + n)
        o += n
    return at, o


def build(nc, x, norm1, w_in, w_gate, w_dt, dt_b, w_x, a_log, dp, w_out, norm2, w_fg, w_fu, w_fd, wg, w1, b1, w2, b2, consts, out):
    B, L, D = x.shape
    DI = w_in.shape[1]
    NS = a_log.shape[2]
    FF = w_fg.shape[1]
    NE, _, H = w1.shape
    S = B * L
    C = S // NE
    NCH = S // T
    PER_BATCH = L // T
    KD, DB, HB = D // P, DI // P, H // P
    FB = -(-FF // P)
    FW = [min(P, FF - P * f) for f in range(FB)]
    assert KD == 2 and DB == 4 and NS == 16 and FB == 6 and NCH % 2 == 0 and NCH >= 4 and L % T == 0 and C % T == 0 and HB == 8

    x_rows = x.rearrange("b l d -> (b l) d")
    out_rows = out.rearrange("b l d -> (b l) d")
    b_scratch = nc.dram_tensor("b_scratch", (2, NS, T), F32, kind="Internal").ap()
    slots_dram = nc.dram_tensor("slots_dram", (S, ROW), F32, kind="Internal").ap()
    at, n_consts = constants_layout(D, NE, NCH)

    def chunk_rows(rows, c):
        return rows[bass.ds(c * T, T), :].rearrange("(t p) d -> p t d", p=P)

    with ExitStack() as ctx:
        def sb(name, shape, dt=F32):
            return ctx.enter_context(nc.sbuf_tensor(name, shape, dt))

        def bank(name, n=1):
            return ctx.enter_context(nc.psum_tensor(name, [P, 512 * n], F32))

        def sem(name):
            return ctx.enter_context(nc.semaphore(name))

        cst = sb("cst", [P, n_consts])
        ident = cst[:, at["ident"][0]:at["ident"][1]]
        rank = cst[:, at["rank"][0]:at["rank"][1]]
        ones_b = sb("ones_b", [P, P], BF16)
        earlier_b = sb("earlier_b", [P, P], BF16)
        w_in_s = sb("w_in_s", [P, KD, DI])
        w_gate_s = sb("w_gate_s", [P, KD, DI])
        w_dt_s = sb("w_dt_s", [P, DB, DI])
        w_x_s = sb("w_x_s", [P, DB, 2 * NS])
        w_out_s = sb("w_out_s", [P, DB, D])
        w_fg_s = sb("w_fg_s", [P, KD, FF])
        w_fu_s = sb("w_fu_s", [P, KD, FF])
        w_fd_s = sb("w_fd_s", [P, FB, D])
        wg_s = sb("wg_s", [P, KD, NE])
        norm1_s = sb("norm1_s", [P, KD])
        norm2_s = sb("norm2_s", [P, KD])
        dt_b_s = sb("dt_b_s", [P, DB])
        dp_s = sb("dp_s", [P, DB])
        A = sb("A", [P, DB, NS])
        eps_rms = sb("eps_rms", [P, 1])
        eps_ln = sb("eps_ln", [P, 1])

        xa = sb("xa", [P, NT, D])
        hT = sb("hT", [P, KD, T])
        z = [sb(f"z{i}", [P, DB, T]) for i in range(2)]
        dt = [sb(f"dt{i}", [P, DB, T]) for i in range(2)]
        u = [sb(f"u{i}", [P, DB, T]) for i in range(2)]
        work = sb("work", [P, DB, T])
        sp_log, sp_fix = work[:, 0:2, :], work[:, 2:4, :]
        bc = sb("bc", [2 * NS, T])
        c_tok = [sb(f"c_tok{i}", [P, NT, NS]) for i in range(2)]
        b_all = sb("b_all", [P, 8, T])
        ub = [sb(f"ub{i}", [P, DB, T]) for i in range(2)]
        h = [sb(f"h{i}", [P, DB, T]) for i in range(2)]
        carry = sb("carry", [P, NS * DB])
        acc = sb("acc", [P, NT, DI])
        xp = sb("xp", [P, NT, D])
        x1 = sb("x1", [P, NT, D])
        hnT = sb("hnT", [P, KD, T])
        gu = sb("gu", [P, FB, T])
        yT = work[:, :, :]
        x1n = work[:, 0:2, :].rearrange("p a (b d) -> p (a b) d", d=D)
        fe = [sb(f"fe{i}", [P, 2, T]) for i in range(2)]
        row = sb("row", [P, NT, ROW])
        row_index = row[:, :, :].bitcast(U32)
        xlT = sb("xlT", [P, KD, T])
        base_out = xlT[:, :, :].rearrange("p a (b d) -> p (a b) d", d=D)

        ss = {s: sb(f"ss_{s}", [P, NT]) for s in "ap"}
        lv = {s: sb(f"lv_{s}", [P, NT]) for s in "aprb"}
        y0 = {s: sb(f"y0_{s}", [P, NT]) for s in "aprb"}
        vv = {s: sb(f"vv_{s}", [P, NT]) for s in "aprb"}
        tt = {s: sb(f"tt_{s}", [P, NT]) for s in "aprb"}
        rs = {s: sb(f"rs_{s}", [P, NT]) for s in "aprb"}
        shift = {s: sb(f"shift_{s}", [P, NT]) for s in "rb"}
        st = {s: sb(f"st_{s}", [P, NT, 6]) for s in "rb"}
        mv = {s: sb(f"mv_{s}", [P, NT, 2]) for s in "rb"}
        lg = sb("lg", [P, NT, NE])
        pe_ = sb("pe_", [P, NT, NE])
        tmp8 = sb("tmp8", [P, NT, NE])
        oh = sb("oh", [P, NT, NE])
        ohb = sb("ohb", [P, NT, NE], BF16)
        filled = sb("filled", [P, NE])
        mx = sb("mx", [P, NT])
        sm = sb("sm", [P, NT])
        pm = sb("pm", [P, NT])
        wm = sb("wm", [P, NT])
        slot_f = sb("slot_f", [P, NT])
        over = sb("over", [P, NT])
        slot_i = sb("slot_i", [P, NT], U32)
        token = sb("token", [P, NT])

        dA = [bank(f"dA{i}") for i in range(3)]
        hB = [bank(f"hB{i}") for i in range(2)]
        aB = bank("aB")
        pB = [bank(f"pB{i}") for i in range(2)]

        names = """small_loaded gates_loaded dt_loaded late_loaded a_ready_first started zeroed zero_tile
            xa_loaded a_ss a_ln a_y0 a_newton a_rs xn_ready a_ready a_free g_clamped g_ln g_ready z_ready b_stored
            sp_exp sp_l sp_m sp_c sp_s dt_ready u_ready ub_ready da_ready scan_done carry_saved ht_ready stt_done
            xp_loaded p_ss p_ln p_y0 p_newton p_rs x1n_ready x1x_ready f_clamped f_ln f_sig ga_ready
            r_stats r_aggr r_ln r_y0 r_newton r_rs r_shift row_ready b_stats b_aggr b_ln b_y0 b_newton b_rs b_shift
            base_ready base_stored probs_ready rt_step oh_ready slot_ready scattered""".split()
        s = {n: sem(n) for n in names}
        p_ready = [sem(f"p_ready{i}") for i in range(2)]
        p_free = [sem(f"p_free{i}") for i in range(2)]
        b_loaded = [sem(f"b_loaded{i}") for i in range(4)]
        passed_sp, passed_pool, passed_dve, passed_pe = (sem(f"passed_{e}") for e in ("sp", "pool", "dve", "pe"))

        STAGES = {"norm": (-2, NCH - 3), "project": (-1, NCH - 2), "scan": (0, NCH - 1), "feed": (1, NCH), "route": (2, NCH + 1)}

        def on(stage, i):
            first, last = STAGES[stage]
            return not isinstance(i, int) or first <= i <= last

        def iterations(eng, iteration):
            for i in range(-2, 2):
                iteration(i, i % 2)
            if NCH > 4:
                with eng.Fori(0, (NCH - 4) // 2) as k:
                    iteration(k * 2 + 2, 0)
                    iteration(k * 2 + 3, 1)
            for i in range(NCH - 2, NCH + 2):
                iteration(i, i % 2)

        A_RING = [(j, "project") for j in ("xT0", "xT1", "gate0", "in0", "gate1", "in1", "gate2", "in2", "gate3", "in3", "bc", "dt0")]
        A_RING += [("xlT0", "route"), ("dt1", "project"), ("xlT1", "route"), ("dt2", "project"), ("dt3", "project"),
                   ("logits", "route"), ("bcT", "project"), ("counts", "route")]
        P_RING = [[(f"acc{b}", "feed"), (f"acc{b + 2}", "feed"), (f"down{b}", "route"), (f"out{b}", "feed"), (f"x1T{b}", "feed")]
                  + [(f"{('gate', 'up')[b]}{f}", "feed") for f in range(FB)] for b in range(2)]

        def before(ring, i, job=None):
            if not isinstance(i, int):
                return i * len(ring) + (before(ring, 2, job) - 2 * len(ring))
            n = sum(on(stage, j) for j in range(-2, i) for _, stage in ring)
            for name, stage in ring:
                if name == job or job is None:
                    break
                n += on(stage, i)
            return n

        def a_count(i, job):
            return before(A_RING, i, job) + 1

        def p_count(b, i, job):
            return before(P_RING[b], i, job) + 1

        def dA_bank(k):
            return 1 if k == NS * DB - 1 else k % 3

        def dA_before(k):
            return next(j for j in range(k - 1, k - 5, -1) if dA_bank(j % (NS * DB)) == dA_bank(k))

        FFN_PE = (38, 40, 42, 44, 46, 47, 49, 50, 52, 53, 55, 57)
        FFN_ACT = (40, 44, 48, 51, 54, 57)
        FFN_DVE = (41, 45, 48, 51, 54, 58)
        block = ctx.enter_context(nc.Block())

        @block.sync
        def _(sp):
            sp.dma_start(xa[:, :, :], chunk_rows(x_rows, 0)).then_inc(s["xa_loaded"], 16)
            for dst, src, done in (
                (cst[:, :], consts, "small_loaded"), (norm1_s[:, :], norm1, "small_loaded"), (norm2_s[:, :], norm2, "small_loaded"),
                (dt_b_s[:, :], dt_b, "small_loaded"), (dp_s[:, :], dp, "small_loaded"), (A[:, :, :], a_log, "small_loaded"),
                (w_gate_s[:, :, :], w_gate.rearrange("(k p) e -> p k e", p=P), "gates_loaded"),
                (w_in_s[:, :, :], w_in.rearrange("(k p) e -> p k e", p=P), "gates_loaded"),
                (w_x_s[:, :, :], w_x.rearrange("(k p) e -> p k e", p=P), "dt_loaded"),
                (w_dt_s[:, :, :], w_dt.rearrange("(k p) e -> p k e", p=P), "dt_loaded"),
                (w_out_s[:, :, :], w_out.rearrange("(k p) e -> p k e", p=P), "late_loaded"),
                (w_fg_s[:, :, :], w_fg.rearrange("(k p) e -> p k e", p=P), "late_loaded"),
                (w_fu_s[:, :, :], w_fu.rearrange("(k p) e -> p k e", p=P), "late_loaded"),
                (w_fd_s[:, 0:FB - 1, :], w_fd[0:P * (FB - 1), :].rearrange("(k p) e -> p k e", p=P), "late_loaded"),
                (w_fd_s[0:FW[-1], FB - 1, :], w_fd[P * (FB - 1):FF, :], "late_loaded"),
                (wg_s[:, :, :], wg.rearrange("(k p) e -> p k e", p=P), "late_loaded"),
            ):
                sp.dma_start(dst, src).then_inc(s[done], 16)

            def iteration(i, par):
                for n in range(NS):
                    if on("norm", i) and n == 1:
                        c = i + 2
                        if not isinstance(c, int) or c > 0:
                            if some(v := a_count(i, "xT1")):
                                sp.wait_ge(s["a_ready"], v)
                                sp.sem_inc(passed_sp, 1)
                            sp.dma_start(xa[:, :, :], chunk_rows(x_rows, c)).then_inc(s["xa_loaded"], 16)
                    if n % 2 == 0:
                        g, c, from_par = (n // 2 + 1, i, par) if n < NS - 2 else (0, i + 1, 1 - par)
                        if on("scan", c):
                            if g == 0:
                                sp.wait_ge(s["b_stored"], (c + 1) * 16)
                                sp.sem_inc(passed_sp, 1)
                            if some(v := c * NS + 2 * g - 6):
                                sp.wait_ge(s["ub_ready"], v)
                                sp.sem_inc(passed_sp, 1)
                            sp.dma_start(b_all[:, 2 * (g % 4):2 * (g % 4) + 2, :],
                                         b_scratch[from_par, 2 * g:2 * g + 2, :].partition_broadcast(P)).then_inc(b_loaded[g % 4], 16)
                    if on("feed", i) and n == 2:
                        c = i - 1
                        if some(v := c):
                            sp.wait_ge(s["x1x_ready"], v)
                            sp.sem_inc(passed_sp, 1)
                        sp.dma_start(xp[:, :, :], chunk_rows(x_rows, c)).then_inc(s["xp_loaded"], 16)
                    if on("project", i) and n == 9:
                        sp.wait_ge(s["a_free"], a_count(i, "bc"))
                        sp.sem_inc(passed_sp, 1)
                        if some(v := i * NS):
                            sp.wait_ge(s["ub_ready"], v)
                            sp.sem_inc(passed_sp, 1)
                        sp.dma_start(b_scratch[1 - par, :, :], bc[0:NS, :]).then_inc(s["b_stored"], 16)
                    if first(i, -1) and n == 12:
                        sp.wait_ge(s["zero_tile"], 2)
                        for g in range(S // T):
                            sp.dma_start(chunk_rows(slots_dram, g), row[:, :, :]).then_inc(s["zeroed"], 16)
                    if on("route", i) and n == NS - 1:
                        c = i - 2
                        sp.wait_ge(s["base_ready"], c + 1)
                        sp.sem_inc(passed_sp, 1)
                        sp.dma_start(chunk_rows(out_rows, c), base_out).then_inc(s["base_stored"], 16)

            iterations(sp, iteration)
            sp.wait_ge(s["base_stored"], 16 * NCH)
            sp.wait_ge(s["scattered"], 16 * NT * NCH)

        @block.gpsimd
        def _(pool):
            def iteration(i, par):
                for n in range(NS):
                    if on("scan", i):
                        c = i
                        if n == 0:
                            pool.wait_ge(s["u_ready"], 2 * c + 2)
                        if n % 2 == 0:
                            pool.wait_ge(b_loaded[(n // 2) % 4], (2 * c + n // 8 + 1) * 16)
                        if some(v := 64 * c + 4 * (n - 1)):
                            pool.wait_ge(s["scan_done"], v)
                        pool.tensor_tensor(ub[n % 2][:, :, :], u[par][:, :, :],
                                           b_all[:, n % 8, :].unsqueeze(1).broadcast_to([P, DB, T]), ALU.mult).then_inc(s["ub_ready"], 1)
                    side(i, par, n)

            def gate_up(c, g):
                pool.wait_ge(s["f_sig"], 3 * c + g + 1)
                pool.wait_ge(p_free[1], p_count(1, c + 1, f"up{2 * g + 1}"))
                pool.tensor_tensor(gu[:, 2 * g:2 * g + 2, :], gu[:, 2 * g:2 * g + 2, :], fe[g % 2][:, :, :], ALU.mult).then_inc(s["ga_ready"], 1)

            def side(i, par, n):
                if on("route", i) and n in (0, 1):
                    gate_up(i - 2, n + 1)
                if on("project", i):
                    c, q = i + 1, 1 - par
                    for half in range(2):
                        d = slice(2 * half, 2 * half + 2)
                        if n == 4 + half:
                            pool.wait_ge(s["g_ready"], 2 * c + half + 1)
                            pool.wait_ge(s["a_free"], a_count(i, f"in{2 * half + 1}"))
                            pool.tensor_tensor(z[q][:, d, :], z[q][:, d, :], u[q][:, d, :], ALU.mult).then_inc(s["z_ready"], 1)
                        if n == (10, 12)[half]:
                            pool.wait_ge(s["sp_m"], 2 * c + half + 1)
                            pool.tensor_tensor(sp_fix, u[q][:, d, :], sp_fix, ALU.subtract).then_inc(s["sp_c"], 1)
                        if n == (11, 13)[half]:
                            pool.wait_ge(s["sp_c"], 2 * c + half + 1)
                            pool.wait_ge(s["sp_l"], 2 * c + half + 1)
                            pool.tensor_tensor(sp_fix, sp_fix, sp_log, ALU.add).then_inc(s["sp_s"], 1)
                        if n == (12, 14)[half]:
                            pool.wait_ge(s["dt_ready"], 2 * c + half + 1)
                            pool.tensor_tensor(u[q][:, d, :], dt[q][:, d, :], z[q][:, d, :], ALU.mult).then_inc(s["u_ready"], 1)
                if on("feed", i):
                    c = i - 1
                    if n == 8:
                        pool.wait_ge(s["xp_loaded"], 16 * (c + 1))
                        pool.wait_ge(s["x1n_ready"], c + 1)
                        pool.tensor_tensor(x1[:, :, :], x1[:, :, :], xp[:, :, :], ALU.add).then_inc(s["x1x_ready"], 1)
                    if n == 13:
                        gate_up(c, 0)
                if on("route", i) and n == 15:
                    c = i - 2
                    pool.wait_ge(s["slot_ready"], c + 1)
                    pool.sem_inc(passed_pool, 1)
                    pool.wait_ge(s["zeroed"], 16 * (S // T))
                    for t in range(NT):
                        pool.indirect_dma_start(out=slots_dram, out_offset=bass.IndirectOffsetOnAxis(slot_i[:, t:t + 1], 0),
                                                in_=row[:, t, :], in_offset=None, bounds_check=S - 1,
                                                oob_is_err=False).then_inc(s["scattered"], 16)

            iterations(pool, iteration)

        @block.scalar
        def _(act):
            act.preload_act_table_set(EXP_LN)
            act.wait_ge(s["small_loaded"], 6 * 16)
            act.activation(A[:, :, :], A[:, :, :], ACT.Exp).then_inc(s["a_ready_first"], 1)
            act.wait_ge(s["started"], 1)

            def start_rsqrt(src, scale, eps, side, ln_done, y0_done, count):
                act.activation(lv[side][:, :], src, ACT.Ln, bias=eps[:, 0:1], scale=scale).then_inc(s[ln_done], 1)
                act.wait_ge(s[ln_done], count)
                act.activation(y0[side][:, :], lv[side][:, :], ACT.Exp, scale=-0.5).then_inc(s[y0_done], 1)

            def iteration(i, par):
                for k in range(NS * DB):
                    if on("scan", i):
                        n, db = k // DB, k % DB
                        if k == 0:
                            act.wait_ge(s["dt_ready"], 2 * i + 2)
                        if some(v := 64 * i + (dA_before(k) + 1)):
                            act.wait_ge(s["scan_done"], v)
                        act.activation(dA[dA_bank(k)][:, :], dt[par][:, db, :], ACT.Exp, scale=A[:, db, n:n + 1]).then_inc(s["da_ready"], 1)
                    if on("norm", i):
                        norm(i, k)
                    if on("project", i):
                        project(i, 1 - par, k)
                    if on("feed", i):
                        feed(i, k)
                    if on("route", i):
                        route(i, k)

            def norm(i, k):
                c = i + 2
                if k == 24:
                    act.wait_ge(s["xa_loaded"], 16 * (c + 1))
                    if some(v := before(A_RING, i, "bc")):
                        act.wait_ge(s["a_ready"], v)
                    for t in range(NT):
                        last = act.activation(hT[:, t // 2, (t % 2) * D:(t % 2 + 1) * D], xa[:, t, :], ACT.Square, accum_out=ss["a"][:, t:t + 1])
                    last.then_inc(s["a_ss"], 1)
                    act.wait_ge(s["a_ss"], c + 1)
                    start_rsqrt(ss["a"][:, :], 1.0 / D, eps_rms, "a", "a_ln", "a_y0", c + 1)
                if k == 29:
                    act.wait_ge(s["a_rs"], c + 1)
                    for t in range(NT):
                        last = act.activation(xa[:, t, :], xa[:, t, :], ACT.Copy, scale=rs["a"][:, t:t + 1])
                    last.then_inc(s["xn_ready"], 1)

            def project(i, q, k):
                c = i + 1
                if k in (1, 3):
                    j = k // 2
                    act.wait_ge(s["a_ready"], a_count(i, f"xT{j}"))
                    act.activation(hT[:, j, :], aB[:, :], ACT.Copy, scale=norm1_s[:, j:j + 1]).then_inc(s["a_free"], 1)
                if 5 <= k <= 19 and k % 2 == 1:
                    d = (k - 5) // 4
                    if k % 4 == 1:
                        if k == 5 and some(v := 16 * i):
                            act.wait_ge(s["ub_ready"], v)
                        act.wait_ge(s["a_ready"], a_count(i, f"gate{d}"))
                        act.activation(u[q][:, d, :], aB[:, :], ACT.Exp, scale=-1.0).then_inc(s["a_free"], 1)
                    else:
                        if on("feed", i) and k == 7:
                            act.wait_ge(p_free[0], p_count(0, i, "acc2"))
                            act.wait_ge(p_free[1], p_count(1, i, "acc3"))
                        act.wait_ge(s["a_ready"], a_count(i, f"in{d}"))
                        act.activation(z[q][:, d, :], aB[:, :], ACT.Copy).then_inc(s["a_free"], 1)
                if k in (12, 20):
                    half = (k - 12) // 8
                    d = slice(2 * half, 2 * half + 2)
                    act.wait_ge(s["g_clamped"], 2 * c + half + 1)
                    act.activation(u[q][:, d, :], u[q][:, d, :], ACT.Ln, bias=1.0).then_inc(s["g_ln"], 1)
                    act.wait_ge(s["g_ln"], 2 * c + half + 1)
                    act.activation(u[q][:, d, :], u[q][:, d, :], ACT.Exp, scale=-1.0).then_inc(s["g_ready"], 1)
                if k == 29:
                    act.wait_ge(s["a_ready"], a_count(i, "bc"))
                    if some(v := 16 * c):
                        act.wait_ge(s["b_stored"], v)
                    act.activation(bc[:, :], aB[0:2 * NS, :], ACT.Copy).then_inc(s["a_free"], 1)
                if k in (32, 37, 42, 45):
                    d = (32, 37, 42, 45).index(k)
                    act.wait_ge(s["z_ready"], 2 * c + 2)
                    act.wait_ge(s["a_ready"], a_count(i, f"dt{d}"))
                    act.activation(dt[q][:, d, :], aB[:, :], ACT.Relu, bias=dt_b_s[:, d:d + 1])
                    act.activation(u[q][:, d, :], aB[:, :], ACT.Abs, bias=dt_b_s[:, d:d + 1]).then_inc(s["a_free"], 1)
                for half in range(2):
                    dd = slice(2 * half, 2 * half + 2)
                    if k == (38, 46)[half]:
                        act.wait_ge(s["a_free"], a_count(i, f"dt{2 * half + 1}"))
                        act.activation(u[q][:, dd, :], u[q][:, dd, :], ACT.Exp, scale=-1.0).then_inc(s["sp_exp"], 1)
                    if k == (39, 47)[half]:
                        act.wait_ge(s["sp_exp"], 2 * c + half + 1)
                        if half == 1:
                            act.wait_ge(s["sp_s"], 2 * c + 1)
                        elif on("feed", i):
                            act.wait_ge(p_ready[0], p_count(0, i, "x1T0"))
                            act.wait_ge(p_ready[1], p_count(1, i, "x1T1"))
                        else:
                            if some(v := 2 * c):
                                act.wait_ge(s["sp_s"], v)
                        act.activation(sp_log, u[q][:, dd, :], ACT.Ln, bias=1.0).then_inc(s["sp_l"], 1)
                if k == 50:
                    act.wait_ge(s["a_ready"], a_count(i, "bcT"))
                    act.activation(c_tok[q][:, :, :], aB[:, 0:NT * 2 * NS].rearrange("p (t m) -> p t m", m=2 * NS)[:, :, NS:2 * NS],
                                   ACT.Copy).then_inc(s["a_free"], 1)

            def feed(i, k):
                c = i - 1
                if k == 28:
                    act.wait_ge(p_free[0], p_count(0, i, "out0"))
                    act.wait_ge(p_free[1], p_count(1, i, "out1"))
                    for t in range(NT):
                        last = act.activation(x1n[:, t, :], x1[:, t, :], ACT.Square, accum_out=ss["p"][:, t:t + 1])
                    last.then_inc(s["p_ss"], 1)
                    act.wait_ge(s["p_ss"], c + 1)
                    start_rsqrt(ss["p"][:, :], 1.0 / D, eps_rms, "p", "p_ln", "p_y0", c + 1)
                if k == 31:
                    act.wait_ge(s["p_rs"], c + 1)
                    for t in range(NT):
                        last = act.activation(x1n[:, t, :], x1[:, t, :], ACT.Copy, scale=rs["p"][:, t:t + 1])
                    last.then_inc(s["x1n_ready"], 1)
                if k in (34, 36):
                    j = (k - 34) // 2
                    act.wait_ge(p_ready[j], p_count(j, i, f"x1T{j}"))
                    act.activation(hnT[:, j, :], pB[j][:, :], ACT.Copy, scale=norm2_s[:, j:j + 1]).then_inc(p_free[j], 1)
                if k in FFN_ACT:
                    f = FFN_ACT.index(k)
                    w = FW[f]
                    act.wait_ge(p_ready[0], p_count(0, i, f"gate{f}"))
                    if f % 2 == 0 and some(v := 3 * c + f // 2 - 1):
                        act.wait_ge(s["ga_ready"], v)
                    if f == 0 and on("route", i):
                        act.wait_ge(p_ready[1], p_count(1, i, "down1"))
                    act.activation(fe[(f // 2) % 2][0:w, f % 2, :], pB[0][0:w, :], ACT.Exp, scale=-1.0)
                    act.activation(gu[0:w, f, :], pB[0][0:w, :], ACT.Copy).then_inc(p_free[0], 1)
                if k in (48, 53, 59):
                    g = (48, 53, 59).index(k)
                    act.wait_ge(s["f_clamped"], 3 * c + g + 1)
                    act.activation(fe[g % 2][:, :, :], fe[g % 2][:, :, :], ACT.Ln, bias=1.0).then_inc(s["f_ln"], 1)
                    act.wait_ge(s["f_ln"], 3 * c + g + 1)
                    act.activation(fe[g % 2][:, :, :], fe[g % 2][:, :, :], ACT.Exp, scale=-1.0).then_inc(s["f_sig"], 1)

            def route(i, k):
                c = i - 2
                if k == 25:
                    act.wait_ge(s["r_aggr"], c + 1)
                    start_rsqrt(mv["r"][:, :, 1], 1.0, eps_ln, "r", "r_ln", "r_y0", c + 1)
                if k == 27:
                    act.wait_ge(s["r_rs"], c + 1)
                    act.wait_ge(s["r_shift"], c + 1)
                    for t in range(NT):
                        last = act.activation(row[:, t, 0:D], row[:, t, 0:D], ACT.Identity, scale=rs["r"][:, t:t + 1], bias=shift["r"][:, t:t + 1])
                    last.then_inc(s["row_ready"], 1)
                if k in (35, 40):
                    j = (k - 35) // 5
                    act.wait_ge(s["a_ready"], a_count(i, f"xlT{j}"))
                    if some(v := 16 * c):
                        act.wait_ge(s["base_stored"], v)
                    act.activation(xlT[:, j, :], aB[:, :], ACT.Copy).then_inc(s["a_free"], 1)
                if k == 49:
                    act.wait_ge(s["a_free"], a_count(i, "logits"))
                    act.activation(pe_[:, :, :], lg[:, :, :], ACT.Exp).then_inc(s["probs_ready"], 1)
                if k == 33:
                    act.wait_ge(s["b_aggr"], c + 1)
                    start_rsqrt(mv["b"][:, :, 1], 1.0, eps_ln, "b", "b_ln", "b_y0", c + 1)
                if k == 55:
                    act.wait_ge(s["b_rs"], c + 1)
                    act.wait_ge(s["b_shift"], c + 1)
                    act.wait_ge(s["a_ready"], a_count(i, "logits"))
                    for t in range(NT):
                        last = act.activation(base_out[:, t, :], row[:, t, 0:D], ACT.Identity, scale=rs["b"][:, t:t + 1], bias=shift["b"][:, t:t + 1])
                    last.then_inc(s["base_ready"], 1)

            iterations(act, iteration)

        @block.vector
        def _(dve):
            dve.memset(eps_rms[:, :], RMS_EPS)
            dve.memset(eps_ln[:, :], LN_EPS)
            dve.memset(carry[:, :], 0.0)
            dve.memset(row[:, :, :], 0.0).then_inc(s["zero_tile"], 1)
            dve.wait_ge(s["zero_tile"], 1)
            dve.tensor_scalar(row_index[:, :, D + 1], row[:, :, D + 1], 1.0, NOWHERE, ALU.mult, ALU.add).then_inc(s["zero_tile"], 1)
            dve.wait_ge(s["small_loaded"], 6 * 16)
            dve.tensor_copy(ones_b[:, :], cst[:, at["ones"][0]:at["ones"][1]])
            dve.tensor_copy(earlier_b[:, :], cst[:, at["earlier"][0]:at["earlier"][1]])
            dve.tensor_copy(filled[:, :], cst[:, at["base"][0]:at["base"][1]])
            dve.tensor_copy(token[:, :], cst[:, at["token"][0]:at["token"][1]])
            dve.memset(gu[:, :, :], 0.0)
            dve.memset(fe[0][:, :, :], 0.0)
            dve.memset(fe[1][:, :, :], 0.0)
            dve.wait_ge(s["a_ready_first"], 1)
            dve.tensor_scalar(A[:, :, :], A[:, :, :], -1.0, None, ALU.mult).then_inc(s["started"], 1)
            dve.wait_ge(s["started"], 1)

            def newton(src, scale, eps, side, y0_done, step, done, c):
                dve.wait_ge(s[y0_done], c + 1)
                dve.tensor_scalar(vv[side][:, :], src, scale, eps, ALU.mult, ALU.add)
                dve.tensor_tensor(tt[side][:, :], y0[side][:, :], y0[side][:, :], ALU.mult).then_inc(s[step], 1)
                dve.wait_ge(s[step], 3 * c + 1)
                dve.tensor_tensor(tt[side][:, :], tt[side][:, :], vv[side][:, :], ALU.mult).then_inc(s[step], 1)
                dve.wait_ge(s[step], 3 * c + 2)
                dve.tensor_scalar(tt[side][:, :], tt[side][:, :], -0.5, 1.5, ALU.mult, ALU.add).then_inc(s[step], 1)
                dve.wait_ge(s[step], 3 * c + 3)
                dve.tensor_tensor(rs[side][:, :], y0[side][:, :], tt[side][:, :], ALU.mult).then_inc(s[done], 1)

            def shifts(side, done, shifted, c):
                dve.wait_ge(s[done], c + 1)
                dve.scalar_tensor_tensor(out=shift[side][:, :], in0=mv[side][:, :, 0], scalar=-1.0, in1=rs[side][:, :],
                                         op0=ALU.mult, op1=ALU.mult).then_inc(s[shifted], 1)

            def iteration(i, par):
                def fold(n, t):
                    dve.wait_ge(s["ht_ready"], 64 * i + 4 * n + t + 1)
                    scalar = c_tok[par][:, t, n:n + 1]
                    if n == 0:
                        ins = dve.tensor_scalar(acc[:, t, :], hB[t % 2][:, :], scalar, None, ALU.mult)
                    else:
                        dve.wait_ge(s["stt_done"], 64 * i + 4 * (n - 1) + t + 1)
                        ins = dve.scalar_tensor_tensor(out=acc[:, t, :], in0=hB[t % 2][:, :], scalar=scalar, in1=acc[:, t, :],
                                                       op0=ALU.mult, op1=ALU.add)
                    ins.then_inc(s["stt_done"], 1)

                def save(n):
                    dve.wait_ge(s["scan_done"], 64 * i + 4 * n + 4)
                    dve.tensor_scalar(carry[:, n * DB:(n + 1) * DB], h[n % 2][:, :, T - 1],
                                      cst[:, bass.ds(i + (at["keep"][0] + 1), 1)], None, ALU.mult).then_inc(s["carry_saved"], 1)

                for k in range(NS * DB):
                    if on("scan", i):
                        n, db = k // DB, k % DB
                        if k == 0:
                            dve.wait_ge(s["a_free"], before(A_RING, i))
                        if db == 0:
                            dve.wait_ge(s["ub_ready"], i * NS + n + 1)
                            if some(v := 64 * i + 4 * (n - 1)):
                                dve.wait_ge(s["ht_ready"], v)
                            if some(v := i * NS + n - 1):
                                dve.wait_ge(s["carry_saved"], v)
                        dve.wait_ge(s["da_ready"], 64 * i + k + 1)
                        dve.tensor_tensor_scan(h[n % 2][:, db, :], dA[dA_bank(k)][:, :], ub[n % 2][:, db, :],
                                               carry[:, k:k + 1], ALU.mult, ALU.add).then_inc(s["scan_done"], 1)
                        if n > 0:
                            fold(n - 1, db)
                            if db == 0:
                                save(n - 1)
                    if on("norm", i) and k == 24:
                        newton(ss["a"][:, :], 1.0 / D, RMS_EPS, "a", "a_y0", "a_newton", "a_rs", i + 2)
                    if on("project", i):
                        project(i, 1 - par, k)
                    if on("feed", i):
                        feed(i, par, k)
                    if on("route", i):
                        route(i, k)
                if on("scan", i):
                    save(NS - 1)
                    for t in range(NT):
                        fold(NS - 1, t)

            def project(i, q, k):
                c = i + 1
                for half in range(2):
                    d = slice(2 * half, 2 * half + 2)
                    if k == (8, 16)[half]:
                        dve.wait_ge(s["a_free"], a_count(i, f"gate{2 * half + 1}"))
                        dve.tensor_scalar(u[q][:, d, :], u[q][:, d, :], EXP_CAP, None, ALU.min).then_inc(s["g_clamped"], 1)
                    if k == (38, 46)[half]:
                        dve.wait_ge(s["sp_exp"], 2 * c + half + 1)
                        if half == 1:
                            dve.wait_ge(s["dt_ready"], 2 * c + 1)
                        elif on("feed", i):
                            dve.wait_ge(p_ready[1], p_count(1, i, "out1"))
                        dve.tensor_scalar(sp_fix, u[q][:, d, :], 1.0, -1.0, ALU.add, ALU.add).then_inc(s["sp_m"], 1)
                    if k == (45, 53)[half]:
                        dve.wait_ge(s["sp_s"], 2 * c + half + 1)
                        dve.wait_ge(s["a_free"], a_count(i, f"dt{2 * half + 1}"))
                        dve.tensor_tensor(dt[q][:, d, :], dt[q][:, d, :], sp_fix, ALU.add).then_inc(s["dt_ready"], 1)

            def feed(i, par, k):
                c = i - 1
                if k < DB:
                    if k == 0 and on("project", i - 1):
                        dve.wait_ge(s["dt_ready"], 2 * i + 2)
                    dve.wait_ge(p_ready[k % 2], p_count(k % 2, i, f"acc{k}"))
                    dve.scalar_tensor_tensor(out=yT[:, k, :], in0=z[1 - par][:, k, :], scalar=dp_s[:, k:k + 1],
                                             in1=pB[k % 2][:, :], op0=ALU.mult, op1=ALU.add).then_inc(p_free[k % 2], 1)
                if k in (22, 25):
                    b = (k - 22) // 3
                    dve.wait_ge(s["xp_loaded"], 16 * (c + 1))
                    dve.wait_ge(p_ready[b], p_count(b, i, f"out{b}"))
                    dve.tensor_tensor(x1[:, 2 * b:2 * b + 2, :], pB[b][:, :].rearrange("p (t d) -> p t d", d=D),
                                      xp[:, 2 * b:2 * b + 2, :], ALU.add).then_inc(p_free[b], 1)
                if k == 27:
                    newton(ss["p"][:, :], 1.0 / D, RMS_EPS, "p", "p_y0", "p_newton", "p_rs", c)
                if k in FFN_DVE:
                    f = FFN_DVE.index(k)
                    w = FW[f]
                    dve.wait_ge(p_free[0], p_count(0, i, f"gate{f}"))
                    dve.wait_ge(p_ready[1], p_count(1, i, f"up{f}"))
                    dve.tensor_tensor(gu[0:w, f, :], pB[1][0:w, :], gu[0:w, f, :], ALU.mult).then_inc(p_free[1], 1)
                if k in (43, 50, 56):
                    g = (43, 50, 56).index(k)
                    dve.wait_ge(p_free[0], p_count(0, i, f"gate{2 * g + 1}"))
                    dve.tensor_scalar(fe[g % 2][:, :, :], fe[g % 2][:, :, :], EXP_CAP, None, ALU.min).then_inc(s["f_clamped"], 1)

            def route(i, k):
                c = i - 2
                if k in (13, 20):
                    b = (k - 13) // 7
                    if k == 13:
                        if first(c, 0):
                            dve.wait_ge(s["zeroed"], 16 * (S // T))
                        if some(v := 64 * c):
                            dve.wait_ge(s["scattered"], v)
                        dve.wait_ge(s["x1x_ready"], c + 1)
                    dve.wait_ge(p_ready[b], p_count(b, i, f"down{b}"))
                    dve.tensor_tensor(row[:, 2 * b:2 * b + 2, 0:D], pB[b][:, :].rearrange("p (t d) -> p t d", d=D),
                                      x1[:, 2 * b:2 * b + 2, :], ALU.add).then_inc(p_free[b], 1)
                if k == 21:
                    dve.wait_ge(p_free[0], p_count(0, i, "down0"))
                    dve.wait_ge(p_free[1], p_count(1, i, "down1"))
                    for t in range(NT):
                        last = dve.bn_stats(st["r"][:, t, :], row[:, t, 0:D])
                    last.then_inc(s["r_stats"], 1)
                if k == 22:
                    dve.wait_ge(s["r_stats"], c + 1)
                    dve.sem_inc(passed_dve, 1)
                    for t in range(NT):
                        last = dve.bn_aggr(mv["r"][:, t, :], st["r"][:, t, :])
                    last.then_inc(s["r_aggr"], 1)
                if k == 24:
                    newton(mv["r"][:, :, 1], 1.0, LN_EPS, "r", "r_y0", "r_newton", "r_rs", c)
                    shifts("r", "r_rs", "r_shift", c)
                if k == 46:
                    dve.wait_ge(s["a_ready"], a_count(i, "logits"))
                    logits = aB[:, 0:NT * NE].rearrange("p (t e) -> p t e", e=NE)
                    dve.tensor_reduce(mx[:, :], logits, AX.X, ALU.max).then_inc(s["rt_step"], 1)
                    dve.wait_ge(s["rt_step"], 9 * c + 1)
                    dve.tensor_tensor(lg[:, :, :], logits, mx[:, :].unsqueeze(2).broadcast_to([P, NT, NE]), ALU.subtract).then_inc(s["a_free"], 1)
                if k == 30:
                    dve.wait_ge(s["row_ready"], c + 1)
                    for t in range(NT):
                        last = dve.bn_stats(st["b"][:, t, :], row[:, t, 0:D])
                    last.then_inc(s["b_stats"], 1)
                if k == 31:
                    dve.wait_ge(s["b_stats"], c + 1)
                    dve.sem_inc(passed_dve, 1)
                    for t in range(NT):
                        last = dve.bn_aggr(mv["b"][:, t, :], st["b"][:, t, :])
                    last.then_inc(s["b_aggr"], 1)
                if k == 48:
                    dve.wait_ge(s["probs_ready"], c + 1)
                    dve.tensor_reduce(sm[:, :], pe_[:, :, :], AX.X, ALU.add)
                    dve.tensor_reduce(pm[:, :], pe_[:, :, :], AX.X, ALU.max).then_inc(s["rt_step"], 1)
                    dve.wait_ge(s["rt_step"], 9 * c + 2)
                    dve.tensor_tensor(tmp8[:, :, :], pe_[:, :, :], pm[:, :].unsqueeze(2).broadcast_to([P, NT, NE]), ALU.is_ge).then_inc(s["rt_step"], 1)
                    dve.reciprocal(sm[:, :], sm[:, :])
                    dve.wait_ge(s["rt_step"], 9 * c + 3)
                    dve.tensor_tensor(tmp8[:, :, :], tmp8[:, :, :], rank.unsqueeze(1).broadcast_to([P, NT, NE]), ALU.mult).then_inc(s["rt_step"], 1)
                    dve.wait_ge(s["rt_step"], 9 * c + 4)
                    dve.tensor_reduce(wm[:, :], tmp8[:, :, :], AX.X, ALU.max).then_inc(s["rt_step"], 1)
                    dve.wait_ge(s["rt_step"], 9 * c + 5)
                    dve.tensor_tensor(row[:, :, D], sm[:, :], pm[:, :], ALU.mult)
                    dve.tensor_tensor(oh[:, :, :], tmp8[:, :, :], wm[:, :].unsqueeze(2).broadcast_to([P, NT, NE]), ALU.is_equal).then_inc(s["rt_step"], 1)
                    dve.wait_ge(s["rt_step"], 9 * c + 6)
                    dve.tensor_copy(ohb[:, :, :], oh[:, :, :]).then_inc(s["oh_ready"], 1)
                    dve.tensor_copy(row_index[:, :, D + 1], token[:, :]).then_inc(s["rt_step"], 1)
                    dve.wait_ge(s["rt_step"], 9 * c + 7)
                    dve.tensor_scalar(token[:, :], token[:, :], float(T), None, ALU.add)
                if k == 55:
                    dve.wait_ge(s["a_ready"], a_count(i, "counts"))
                    counts = aB[:, 0:NT * NE].rearrange("p (t e) -> p t e", e=NE)
                    dve.tensor_tensor(tmp8[:, :, :], counts, filled[:, :].unsqueeze(1).broadcast_to([P, NT, NE]), ALU.add).then_inc(s["rt_step"], 1)
                    dve.wait_ge(s["rt_step"], 9 * c + 8)
                    dve.tensor_tensor(filled[:, :], filled[:, :], aB[:, NT * NE:NT * NE + NE], ALU.add).then_inc(s["a_free"], 1)
                    dve.tensor_tensor(tmp8[:, :, :], tmp8[:, :, :], oh[:, :, :], ALU.mult).then_inc(s["rt_step"], 1)
                    dve.wait_ge(s["rt_step"], 9 * c + 9)
                    dve.tensor_reduce(slot_f[:, :], tmp8[:, :, :], AX.X, ALU.add).then_inc(s["oh_ready"], 1)
                    dve.wait_ge(s["oh_ready"], 5 * c + 2)
                    dve.scalar_tensor_tensor(out=over[:, :], in0=wm[:, :], scalar=float(C), in1=slot_f[:, :], op0=ALU.mult, op1=ALU.add).then_inc(s["oh_ready"], 1)
                    dve.wait_ge(s["oh_ready"], 5 * c + 3)
                    dve.tensor_scalar(over[:, :], over[:, :], float(C * (NE + 1)), NOWHERE, ALU.is_ge, ALU.mult).then_inc(s["oh_ready"], 1)
                    dve.wait_ge(s["oh_ready"], 5 * c + 4)
                    dve.tensor_tensor(slot_f[:, :], slot_f[:, :], over[:, :], ALU.add).then_inc(s["oh_ready"], 1)
                    dve.wait_ge(s["oh_ready"], 5 * c + 5)
                    dve.tensor_copy(slot_i[:, :], slot_f[:, :]).then_inc(s["slot_ready"], 1)
                if k == 34:
                    newton(mv["b"][:, :, 1], 1.0, LN_EPS, "b", "b_y0", "b_newton", "b_rs", c)
                    shifts("b", "b_rs", "b_shift", c)

            iterations(dve, iteration)

        @block.tensor
        def _(pe):
            pe.wait_ge(s["small_loaded"], 6 * 16)
            pe.wait_ge(s["started"], 1)
            pe.wait_ge(s["gates_loaded"], 2 * 16)

            def transposes(to, tiles, done, rows=P):
                for k, tile in enumerate(tiles):
                    last = pe.matmul(to[:, k * rows:(k + 1) * rows], tile, ident[0:rows, 0:rows], start=True, stop=True, is_transpose=True)
                last.then_inc(done, 1)

            def product(to, pairs, steps, of, done=None):
                for k, (lhsT, rhs) in zip(steps, pairs):
                    last = pe.matmul(to, lhsT, rhs, start=(k == 0), stop=(k == of - 1))
                if done is not None:
                    last.then_inc(done, 1)

            def iteration(i, par):
                def turn(n, t):
                    if t == 0:
                        pe.wait_ge(s["scan_done"], 64 * i + 4 * n + 4)
                    if some(v := 64 * i + 4 * n + t - 1):
                        pe.wait_ge(s["stt_done"], v)
                    transposes(hB[t % 2], [h[n % 2][:, db, t * P:(t + 1) * P] for db in range(DB)], s["ht_ready"])

                for k in range(NS * DB):
                    if on("feed", i):
                        feed(i, k)
                    if on("project", i):
                        project(i, 1 - par, k)
                    if on("route", i):
                        route(i, k)
                    if on("scan", i) and k >= DB:
                        turn(k // DB - 1, k % DB)
                if on("scan", i):
                    for t in range(NT):
                        turn(NS - 1, t)

            def project(i, q, k):
                c = i + 1
                if k in (0, 2):
                    j = k // 2
                    pe.wait_ge(s["xn_ready"], c + 1)
                    if some(v := before(A_RING, i, f"xT{j}")):
                        pe.wait_ge(s["a_free"], v)
                    transposes(aB, [xa[:, t, j * P:(j + 1) * P] for t in range(NT)], s["a_ready"])
                if 3 <= k <= 17 and k % 2 == 1:
                    d = (k - 3) // 4
                    name, w = ("gate", w_gate_s) if k % 4 == 3 else ("in", w_in_s)
                    pe.wait_ge(s["a_free"], before(A_RING, i, f"{name}{d}"))
                    product(aB[:, :], [(w[:, j, d * P:(d + 1) * P], hT[:, j, :]) for j in range(KD)], range(KD), KD, s["a_ready"])
                if k in (26, 27):
                    j = 2 * (k - 26)
                    if j == 0:
                        if first(c, 0):
                            pe.wait_ge(s["dt_loaded"], 2 * 16)
                        pe.wait_ge(s["a_free"], before(A_RING, i, "bc"))
                    pe.wait_ge(s["z_ready"], 2 * c + 1 + j // 2)
                    product(aB[0:2 * NS, :], [(w_x_s[:, m, :], z[q][:, m, :]) for m in (j, j + 1)], (j, j + 1), DB, s["a_ready"] if j else None)
                for d, at_k in enumerate(((29, 30), (34, 35), (39, 40), (42, 43))):
                    if k in at_k:
                        j = 2 * at_k.index(k)
                        if j == 0:
                            pe.wait_ge(s["a_free"], before(A_RING, i, f"dt{d}"))
                        product(aB[:, :], [(w_dt_s[:, m, d * P:(d + 1) * P], z[q][:, m, :]) for m in (j, j + 1)], (j, j + 1), DB,
                                s["a_ready"] if j else None)
                if k == 48:
                    pe.wait_ge(s["a_free"], before(A_RING, i, "bcT"))
                    pe.sem_inc(passed_pe, 1)
                    transposes(aB, [bc[:, t * P:(t + 1) * P] for t in range(NT)], s["a_ready"], 2 * NS)

            def feed(i, k):
                c = i - 1
                if k < DB:
                    if k == 0:
                        pe.wait_ge(s["stt_done"], 64 * (c + 1))
                    if some(v := before(P_RING[k % 2], i, f"acc{k}")):
                        pe.wait_ge(p_free[k % 2], v)
                    transposes(pB[k % 2], [acc[:, t, k * P:(k + 1) * P] for t in range(NT)], p_ready[k % 2])
                if k in (20, 21, 23, 24):
                    t = (20, 21, 23, 24).index(k)
                    b = t // 2
                    if k == 20:
                        if first(c, 0):
                            pe.wait_ge(s["late_loaded"], 6 * 16)
                        pe.wait_ge(p_free[1], p_count(1, i, "acc3"))
                    if t % 2 == 0:
                        pe.wait_ge(p_free[b], before(P_RING[b], i, f"out{b}"))
                    product(pB[b][:, (t % 2) * D:(t % 2 + 1) * D], [(yT[:, j, t * P:(t + 1) * P], w_out_s[:, j, :]) for j in range(DB)],
                            range(DB), DB, p_ready[b] if t % 2 else None)
                if k in (32, 34):
                    j = (k - 32) // 2
                    pe.wait_ge(s["x1n_ready"], c + 1)
                    pe.wait_ge(p_free[j], before(P_RING[j], i, f"x1T{j}"))
                    transposes(pB[j], [x1n[:, t, j * P:(j + 1) * P] for t in range(NT)], p_ready[j])
                if k in FFN_PE:
                    f, up = FFN_PE.index(k) // 2, FFN_PE.index(k) % 2
                    if k == FFN_PE[0]:
                        pe.wait_ge(p_free[1], p_count(1, i, "x1T1"))
                    pe.wait_ge(p_free[up], before(P_RING[up], i, f"{('gate', 'up')[up]}{f}"))
                    w = w_fu_s if up else w_fg_s
                    product(pB[up][0:FW[f], :], [(w[:, j, f * P:f * P + FW[f]], hnT[:, j, :]) for j in range(KD)], range(KD), KD, p_ready[up])

            def route(i, k):
                c = i - 2
                if k in (6, 8, 10, 12, 14, 16, 18, 19):
                    n = (6, 8, 10, 12, 14, 16, 18, 19).index(k)
                    t, later = n // 2, n % 2
                    b = t // 2
                    if n < 2:
                        pe.wait_ge(s["ga_ready"], 3 * c + 2 + later)
                    if n % 4 == 0:
                        pe.wait_ge(p_free[b], before(P_RING[b], i, f"down{b}"))
                    fs = range(3 * later, 3 * later + 3)
                    product(pB[b][:, (t % 2) * D:(t % 2 + 1) * D],
                            [(gu[0:FW[f], f, t * P:(t + 1) * P], w_fd_s[0:FW[f], f, :]) for f in fs], fs, FB, p_ready[b] if n % 4 == 3 else None)
                if k in (32, 37):
                    j = (k - 32) // 5
                    pe.wait_ge(s["row_ready"], c + 1)
                    pe.wait_ge(s["a_free"], before(A_RING, i, f"xlT{j}"))
                    transposes(aB, [row[:, t, j * P:(j + 1) * P] for t in range(NT)], s["a_ready"])
                if k == 45:
                    pe.wait_ge(s["a_free"], before(A_RING, i, "logits"))
                    for t in range(NT):
                        product(aB[:, t * NE:(t + 1) * NE], [(xlT[:, j, t * P:(t + 1) * P], wg_s[:, j, :]) for j in range(KD)],
                                range(KD), KD, s["a_ready"] if t == NT - 1 else None)
                if k == 54:
                    pe.wait_ge(s["a_free"], before(A_RING, i, "counts"))
                    pe.wait_ge(s["oh_ready"], 5 * c + 1)
                    for t in range(NT):
                        product(aB[:, t * NE:(t + 1) * NE],
                                [(ones_b[:, :], ohb[:, j, :]) for j in range(t)] + [(earlier_b[:, :], ohb[:, t, :])], range(t + 1), t + 1)
                    product(aB[:, NT * NE:NT * NE + NE], [(ones_b[:, :], ohb[:, j, :]) for j in range(NT)], range(NT), NT, s["a_ready"])

            iterations(pe, iteration)

    with ExitStack() as ctx:
        def sb(name, shape, dt=F32):
            return ctx.enter_context(nc.sbuf_tensor(name, shape, dt))

        def bank(name):
            return ctx.enter_context(nc.psum_tensor(name, [P, 512], F32))

        G = C // T
        NG = NE * G
        TURN = max(2 * G, 4)
        ident2 = sb("ident2", [P, P])
        eps2 = sb("eps2", [P, 1])
        w1_s = [sb(f"w1_{i}", [P, KD, H]) for i in range(2)]
        w2_s = [sb(f"w2_{i}", [P, HB, D]) for i in range(2)]
        b1_s = [sb(f"b1_{i}", [P, HB]) for i in range(2)]
        b2_s = [sb(f"b2_{i}", [P, D]) for i in range(2)]
        rows = [sb(f"rows{i}", [P, NT, ROW]) for i in range(TURN)]
        xeT = [sb(f"xeT{i}", [P, KD, T]) for i in range(2)]
        h1 = [sb(f"h1_{i}", [P, HB, T]) for i in range(2)]
        y = [sb(f"y{i}", [P, NT, D]) for i in range(2)]
        st2 = sb("st2", [P, NT, 6])
        mv2 = sb("mv2", [P, NT, 2])
        lv2, y02, vv2, tt2, rs2 = (sb(f"{n}2", [P, NT]) for n in ("lv", "y0", "vv", "tt", "rs"))
        x_bank = [bank(f"x_bank{i}") for i in range(2)]
        h_bank = [bank(f"h_bank{i}") for i in range(2)]
        o_bank = [bank(f"o_bank{i}") for i in range(2)]
        s = {n: ctx.enter_context(nc.semaphore(n)) for n in """m_const m_eps xt_ready xt_free hid_ready hid_free
            o_ready o_free y_ready y_stats y_aggr y_ln y_y0 y_newton y_rs yn_ready""".split()}
        w_loaded = [ctx.enter_context(nc.semaphore(f"w_loaded{i}")) for i in range(2)]
        rows_loaded = [ctx.enter_context(nc.semaphore(f"rows_loaded{i}")) for i in range(TURN)]
        passed_sp, passed_pool, passed_dve = (ctx.enter_context(nc.semaphore(f"passed2_{e}")) for e in ("sp", "pool", "dve"))
        out_stored = [ctx.enter_context(nc.semaphore(f"out_stored{i}")) for i in range(TURN)]
        assert NG % TURN == 0 and TURN % (2 * G) == 0 and NG > TURN
        block = ctx.enter_context(nc.Block())

        def groups(eng, one):
            def turn(k):
                for j in range(TURN):
                    e = j // G
                    one(k * (TURN // G) + e, e % 2, k * TURN + j, j, k, k * (TURN // G // 2) + e // 2 + 1, j % G == 0)

            turn(0)
            with eng.Fori(1, NG // TURN) as k:
                turn(k)

        @block.sync
        def _(sp):
            sp.dma_start(ident2[:, :], consts[:, at["ident"][0]:at["ident"][1]]).then_inc(s["m_const"], 16)

            def one(e, ep, g, j, k, fills, opens):
                if opens:
                    if some(v := (e - 1) * (2 * G)):
                        sp.wait_ge(s["o_free"], v)
                        sp.sem_inc(passed_sp, 1)
                    for dst, src in ((w1_s[ep][:, :, :], w1[bass.ds(e, 1), :, :].rearrange("o (k p) h -> p (o k) h", p=P)),
                                     (w2_s[ep][:, :, :], w2[bass.ds(e, 1), :, :].rearrange("o (k p) d -> p (o k) d", p=P)),
                                     (b1_s[ep][:, :], b1[bass.ds(e, 1), :, :].rearrange("o p k -> p (o k)")),
                                     (b2_s[ep][:, :], b2[bass.ds(e, 1), :].rearrange("o d -> (o d)").partition_broadcast(P))):
                        sp.dma_start(dst, src).then_inc(w_loaded[ep], 16)
                if some(v := k * (16 * NT)):
                    sp.wait_ge(out_stored[j], v)
                    sp.sem_inc(passed_sp, 1)
                sp.dma_start(rows[j][:, :, :], chunk_rows(slots_dram, g)).then_inc(rows_loaded[j], 16)

            groups(sp, one)
            for j in range(TURN):
                sp.wait_ge(out_stored[j], (NG // TURN) * 16 * NT)

        @block.tensor
        def _(pe):
            pe.wait_ge(s["m_const"], 16)

            def down(g, gp, ep):
                for m in range(2):
                    pe.wait_ge(s["hid_free"], HB * g + HB)
                    if some(v := 2 * g + m - 1):
                        pe.wait_ge(s["o_free"], v)
                    for i in range(2):
                        t = 2 * m + i
                        for f in range(HB):
                            last = pe.matmul(o_bank[m][:, i * D:(i + 1) * D], h1[gp][:, f, t * P:(t + 1) * P], w2_s[ep][:, f, :],
                                             start=(f == 0), stop=(f == HB - 1))
                    last.then_inc(s["o_ready"], 1)

            def one(e, ep, g, j, k, fills, opens):
                gp = j % 2
                pe.wait_ge(rows_loaded[j], k * 16 + 16)
                for kd in range(KD):
                    if some(v := 2 * g + kd - 1):
                        pe.wait_ge(s["xt_free"], v)
                    for t in range(NT):
                        last = pe.matmul(x_bank[kd][:, t * P:(t + 1) * P], rows[j][:, t, kd * P:(kd + 1) * P], ident2[:, :],
                                         start=True, stop=True, is_transpose=True)
                    last.then_inc(s["xt_ready"], 1)
                pe.wait_ge(w_loaded[ep], fills * 64)
                pe.wait_ge(s["xt_free"], 2 * g + 2)
                for f in range(HB):
                    if some(v := HB * g + f - 1):
                        pe.wait_ge(s["hid_free"], v)
                    for kd in range(KD):
                        last = pe.matmul(h_bank[f % 2][:, :], w1_s[ep][:, kd, f * P:(f + 1) * P], xeT[gp][:, kd, :],
                                         start=(kd == 0), stop=(kd == KD - 1))
                    last.then_inc(s["hid_ready"], 1)
                if not isinstance(g, int) or g > 0:
                    down(g - 1, 1 - gp, 1 - ep if opens else ep)

            groups(pe, one)
            down(NG - 1, 1, 1)

        @block.scalar
        def _(act):
            act.preload_act_table_set(EXP_LN)
            act.wait_ge(s["m_eps"], 1)

            def norm(g):
                act.wait_ge(s["y_aggr"], g + 1)
                act.activation(lv2[:, :], mv2[:, :, 1], ACT.Ln, bias=eps2[:, 0:1]).then_inc(s["y_ln"], 1)
                act.wait_ge(s["y_ln"], g + 1)
                act.activation(y02[:, :], lv2[:, :], ACT.Exp, scale=-0.5).then_inc(s["y_y0"], 1)

            def one(e, ep, g, j, k, fills, opens):
                gp = j % 2
                for kd in range(KD):
                    act.wait_ge(s["xt_ready"], 2 * g + kd + 1)
                    act.activation(xeT[gp][:, kd, :], x_bank[kd][:, :], ACT.Copy).then_inc(s["xt_free"], 1)
                act.wait_ge(w_loaded[ep], fills * 64)
                for f in range(HB):
                    act.wait_ge(s["hid_ready"], HB * g + f + 1)
                    act.activation(h1[gp][:, f, :], h_bank[f % 2][:, :], ACT.Relu, bias=b1_s[ep][:, f:f + 1]).then_inc(s["hid_free"], 1)
                    if f == 2 and (not isinstance(g, int) or g > 1):
                        norm(g - 2)

            groups(act, one)
            norm(NG - 2)
            norm(NG - 1)

        @block.vector
        def _(dve):
            dve.memset(eps2[:, :], LN_EPS).then_inc(s["m_eps"], 1)

            def one(e, ep, g, j, k, fills, opens):
                gp = j % 2
                dve.wait_ge(w_loaded[ep], fills * 64)
                if not isinstance(g, int) or g >= 2:
                    dve.wait_ge(out_stored[(j - 2) % TURN], k * (16 * NT) + (16 * NT if j >= 2 else 0))
                for m in range(2):
                    dve.wait_ge(s["o_ready"], 2 * g + m + 1)
                    dve.tensor_tensor(y[gp][:, 2 * m:2 * m + 2, :], o_bank[m][:, :].rearrange("p (t d) -> p t d", d=D),
                                      b2_s[ep][:, :].unsqueeze(1).broadcast_to([P, 2, D]), ALU.add).then_inc(s["o_free"], 1)
                dve.wait_ge(s["o_free"], 2 * g + 2)
                for t in range(NT):
                    last = dve.scalar_tensor_tensor(out=y[gp][:, t, :], in0=y[gp][:, t, :], scalar=rows[j][:, t, D:D + 1],
                                                    in1=rows[j][:, t, 0:D], op0=ALU.mult, op1=ALU.add)
                last.then_inc(s["y_ready"], 1)
                dve.wait_ge(s["y_ready"], g + 1)
                for t in range(NT):
                    last = dve.bn_stats(st2[:, t, :], y[gp][:, t, :])
                last.then_inc(s["y_stats"], 1)
                dve.wait_ge(s["y_stats"], g + 1)
                dve.sem_inc(passed_dve, 1)
                for t in range(NT):
                    last = dve.bn_aggr(mv2[:, t, :], st2[:, t, :])
                last.then_inc(s["y_aggr"], 1)
                dve.wait_ge(s["y_y0"], g + 1)
                dve.tensor_scalar(vv2[:, :], mv2[:, :, 1], 1.0, LN_EPS, ALU.mult, ALU.add)
                dve.tensor_tensor(tt2[:, :], y02[:, :], y02[:, :], ALU.mult).then_inc(s["y_newton"], 1)
                dve.wait_ge(s["y_newton"], 3 * g + 1)
                dve.tensor_tensor(tt2[:, :], tt2[:, :], vv2[:, :], ALU.mult).then_inc(s["y_newton"], 1)
                dve.wait_ge(s["y_newton"], 3 * g + 2)
                dve.tensor_scalar(tt2[:, :], tt2[:, :], -0.5, 1.5, ALU.mult, ALU.add).then_inc(s["y_newton"], 1)
                dve.wait_ge(s["y_newton"], 3 * g + 3)
                dve.tensor_tensor(rs2[:, :], y02[:, :], tt2[:, :], ALU.mult).then_inc(s["y_rs"], 1)
                dve.wait_ge(s["y_rs"], g + 1)
                for t in range(NT):
                    last = dve.tensor_scalar(y[gp][:, t, :], y[gp][:, t, :], mv2[:, t, 0:1], rs2[:, t:t + 1], ALU.subtract, ALU.mult)
                last.then_inc(s["yn_ready"], 1)

            groups(dve, one)

        @block.gpsimd
        def _(pool):
            def one(e, ep, g, j, k, fills, opens):
                pool.wait_ge(s["yn_ready"], g + 1)
                pool.sem_inc(passed_pool, 1)
                for t in range(NT):
                    pool.indirect_dma_start(out=out_rows, out_offset=bass.IndirectOffsetOnAxis(rows[j][:, :, :].bitcast(U32)[:, t, D + 1:D + 2], 0),
                                            in_=y[j % 2][:, t, :], in_offset=None, bounds_check=S - 1,
                                            oob_is_err=False).then_inc(out_stored[j], 16)

            groups(pool, one)

    return nc


def kernel(**inputs):
    import numpy as np
    import concourse.bacc as bacc
    from concourse.bass_utils import run_bass_kernel_spmd

    a = {k.replace("L0_attn_", "").replace("L0_ffn_", "moe_"): np.asarray(v) for k, v in inputs.items()}
    B, L, D = a["x"].shape
    NE, _, H = a["moe_w1"].shape
    DI, NS = a["A_log"].shape
    S = B * L
    NCH = S // T
    at, n_consts = constants_layout(D, NE, NCH)

    consts = np.zeros((P, n_consts), np.float32)
    for name, table in (
        ("ident", np.eye(P)),
        ("earlier", np.triu(np.ones((P, P)), 1)),
        ("ones", np.ones((P, P))),
        ("rank", NE - np.arange(NE)[None]),
        ("base", (S // NE) * np.arange(NE)[None]),
        ("keep", (np.arange(NCH + 1) % (L // T) != 0)[None]),
        ("token", np.arange(P)[:, None] + P * np.arange(NT)[None]),
    ):
        consts[:, at[name][0]:at[name][1]] = table

    def by_partition(v):
        return v.reshape(-1, P).T

    arrays = dict(
        x=a["x"], norm1=by_partition(a["norm1_w"]), w_in=a["in_proj_w"].T, w_gate=a["gate_proj_w"].T, w_dt=a["dt_w"].T,
        dt_b=by_partition(a["dt_b"]), w_x=a["x_proj_w"].T, a_log=a["A_log"].reshape(DI // P, P, NS).transpose(1, 0, 2),
        dp=by_partition(a["Dp"]), w_out=a["out_proj_w"].T, norm2=by_partition(a["ffn_norm_w"]),
        w_fg=a["ffn_gate_w"].T, w_fu=a["ffn_up_w"].T, w_fd=a["ffn_down_w"].T,
        wg=a["moe_wg"], w1=a["moe_w1"], b1=a["moe_b1"].reshape(NE, H // P, P).transpose(0, 2, 1), w2=a["moe_w2"], b2=a["moe_b2"],
        consts=consts,
    )
    nc = bacc.Bacc("TRN2", target_bir_lowering=False, num_devices=1)
    feeds, args = {}, []
    for name, v in arrays.items():
        v = np.ascontiguousarray(v)
        feeds[f"in_{name}"] = v
        args.append(nc.dram_tensor(f"in_{name}", v.shape, mybir.dt.from_np(v.dtype), kind="ExternalInput").ap())
    args.append(nc.dram_tensor("out_0", (B, L, D), F32, kind="ExternalOutput").ap())
    build(nc, *args)
    r = run_bass_kernel_spmd(nc, [feeds], core_ids=[0])
    return r.results[0]["out_0"]
```

```python
from contextlib import ExitStack

import concourse.bass as bass
from concourse import mybir
from concourse.alu_op_type import AluOpType as ALU

F32 = mybir.dt.float32
F32R = mybir.dt.float32r
BF16 = mybir.dt.bfloat16
U32 = mybir.dt.uint32
ACT = mybir.ActivationFunctionType
AX = mybir.AxisListType

P = 128
T = 512
NT = T // P
ROW = 260
RMS_EPS = 1e-6
LN_EPS = 1e-5
EXP_CAP = 1e18
NOWHERE = 65536.0
EXP_LN = "natural_log_exp_and_others"


STEPS = dict(
    pe_xT=(0, 1),
    pe_gate_in=(4, 6, 8, 10, 12, 14, 16, 17),
    pe_bc=(26, 27),
    pe_dt=(29, 30, 34, 35, 39, 40, 42, 43),
    pe_bcT=48,
    pe_out=(20, 21, 23, 24),
    pe_x1T=(31, 34),
    pe_gate_up=(36, 38, 42, 44, 46, 47, 49, 50, 52, 53, 55, 57),
    pe_down=(6, 8, 10, 12, 14, 16, 18, 19),
    pe_xlT=(33, 37),
    pe_logits=46,
    pe_counts=51,
    act_ss=23,
    act_xn=26,
    act_hT=(2, 3),
    act_gate_in=(4, 7, 10, 12, 14, 15, 18, 20),
    act_sigmoid=(14, 19),
    act_bc=28,
    act_dt=(32, 37, 42, 45),
    act_e=(37, 46),
    act_ln=(38, 47),
    act_c_tok=50,
    act_p_ss=28,
    act_x1n=31,
    act_hnT=(33, 36),
    act_gate=(38, 44, 46, 51, 54, 57),
    act_ffn_sigmoid=(45, 52, 59),
    act_r_rsqrt=22,
    act_row=25,
    act_xlT=(33, 37),
    act_probs=49,
    act_b_rsqrt=33,
    act_base=55,
    act_first_fold=6,
    act_save=3,
    dve_a_newton=23,
    dve_cap=(9, 16),
    dve_rounded=(37, 46),
    dve_dt=(44, 49),
    dve_x1=(24, 25),
    dve_p_newton=28,
    dve_gate_up=(39, 45, 48, 51, 54, 58),
    dve_ffn_cap=(43, 49, 55),
    dve_row=(12, 18),
    dve_r_stats=19,
    dve_r_aggr=20,
    dve_r_newton=22,
    dve_b_stats=27,
    dve_b_aggr=31,
    dve_b_newton=33,
    dve_logits=45,
    dve_choice=48,
    dve_slot=52,
    pool_z=(5, 6),
    pool_lost=(10, 12),
    pool_sum=(11, 12),
    pool_u=(12, 14),
    pool_x1x=8,
    pool_ga0=13,
    pool_scatter=15,
)


def some(count):
    return not isinstance(count, int) or count > 0


def first(count, start):
    return isinstance(count, int) and count == start


def constants_layout(D, NE, NCH):
    columns, o = {}, 0
    for name, n in (("ident", P), ("earlier", P), ("ones", P), ("rank", NE), ("base", NE), ("keep", NCH + 1), ("token", NT)):
        columns[name] = (o, o + n)
        o += n
    return columns, o


def build(nc, x, norm1, w_in, w_gate, w_dt, dt_b, w_x, a_log, dp, w_out, norm2, w_fg, w_fu, w_fd, wg, w1, b1, w2, b2, consts, out):
    B, L, D = x.shape
    DI = w_in.shape[1]
    NS = a_log.shape[2]
    FF = w_fg.shape[1]
    NE, _, H = w1.shape
    S = B * L
    C = S // NE
    NCH = S // T
    PER_BATCH = L // T
    KD, DB, HB = D // P, DI // P, H // P
    FB = -(-FF // P)
    FW = [min(P, FF - P * f) for f in range(FB)]
    assert KD == 2 and DB == 4 and NS == 16 and FB == 6 and NCH % 2 == 0 and NCH >= 4 and L % T == 0 and C % T == 0 and HB == 8

    x_rows = x.rearrange("b l d -> (b l) d")
    out_rows = out.rearrange("b l d -> (b l) d")
    b_scratch = nc.dram_tensor("b_scratch", (2, NS, T), F32, kind="Internal").ap()
    slots_dram = nc.dram_tensor("slots_dram", (S, ROW), F32, kind="Internal").ap()
    columns, n_consts = constants_layout(D, NE, NCH)

    def chunk_rows(rows, c):
        return rows[bass.ds(c * T, T), :].rearrange("(t p) d -> p t d", p=P)

    with ExitStack() as both:
        cst = both.enter_context(nc.sbuf_tensor("cst", [P, n_consts], F32))
        ident = cst[:, columns["ident"][0]:columns["ident"][1]]
        eps_ln = both.enter_context(nc.sbuf_tensor("eps_ln", [P, 1], F32))
        b_all = both.enter_context(nc.sbuf_tensor("b_all", [P, 8, T], F32))
        w1_stage = b_all[:, 0:4, :].rearrange("p a t -> p (a t)").rearrange("p (k h) -> p k h", k=KD)
        w2_stage = b_all[:, 4:8, :].rearrange("p a t -> p (a t)").rearrange("p (k d) -> p k d", k=HB)
        w1_loaded, w2_loaded = both.enter_context(nc.semaphore("w1_loaded")), both.enter_context(nc.semaphore("w2_loaded"))

        def load_w1(sp, e):
            sp.dma_start(w1_stage, w1[bass.ds(e, 1), :, :].rearrange("o (k p) h -> p (o k) h", p=P)).then_inc(w1_loaded, 16)

        def load_w2(sp, e):
            sp.dma_start(w2_stage, w2[bass.ds(e, 1), :, :].rearrange("o (k p) d -> p (o k) d", p=P)).then_inc(w2_loaded, 16)

        with ExitStack() as ctx:
            def sb(name, shape, dt=F32):
                return ctx.enter_context(nc.sbuf_tensor(name, shape, dt))

            def bank(name, n=1):
                return ctx.enter_context(nc.psum_tensor(name, [P, 512 * n], F32))

            def sem(name):
                return ctx.enter_context(nc.semaphore(name))

            rank = cst[:, columns["rank"][0]:columns["rank"][1]]
            ones_b = sb("ones_b", [P, P], BF16)
            earlier_b = sb("earlier_b", [P, P], BF16)
            w_in_s = sb("w_in_s", [P, KD, DI])
            w_gate_s = sb("w_gate_s", [P, KD, DI])
            w_dt_s = sb("w_dt_s", [P, DB, DI])
            w_x_s = sb("w_x_s", [P, DB, 2 * NS])
            w_out_s = sb("w_out_s", [P, DB, D])
            w_fg_s = sb("w_fg_s", [P, KD, FF])
            w_fu_s = sb("w_fu_s", [P, KD, FF])
            w_fd_s = sb("w_fd_s", [P, FB, D])
            wg_s = sb("wg_s", [P, KD, NE])
            norm1_s = sb("norm1_s", [P, KD])
            norm2_s = sb("norm2_s", [P, KD])
            dt_b_s = sb("dt_b_s", [P, DB])
            dp_s = sb("dp_s", [P, DB])
            A = sb("A", [P, DB, NS])
            eps_rms = sb("eps_rms", [P, 1])

            xa = sb("xa", [P, NT, D])
            hT = sb("hT", [P, KD, T])
            z = [sb(f"z{i}", [P, DB, T]) for i in range(2)]
            dt = [sb(f"dt{i}", [P, DB, T]) for i in range(2)]
            u = [sb(f"u{i}", [P, DB, T]) for i in range(2)]
            work = sb("work", [P, DB, T])
            sp_log, sp_fix = work[:, 0:2, :], work[:, 2:4, :]
            bc = sb("bc", [2 * NS, T])
            c_tok = [sb(f"c_tok{i}", [P, NT, NS]) for i in range(2)]
            ub = [sb(f"ub{i}", [P, DB, T]) for i in range(2)]
            h = [sb(f"h{i}", [P, DB, T]) for i in range(2)]
            carry = sb("carry", [P, NS * DB])
            acc = sb("acc", [P, NT, DI])
            xp = sb("xp", [P, NT, D])
            x1 = sb("x1", [P, NT, D])
            hnT = sb("hnT", [P, KD, T])
            gu = sb("gu", [P, FB, T])
            yT = work[:, :, :]
            x1n = work[:, 0:2, :].rearrange("p a (b d) -> p (a b) d", d=D)
            fe = [sb(f"fe{i}", [P, 2, T]) for i in range(2)]
            row = sb("row", [P, NT, ROW])
            row_index = row[:, :, :].bitcast(U32)
            xlT = sb("xlT", [P, KD, T])
            base_out = xlT[:, :, :].rearrange("p a (b d) -> p (a b) d", d=D)

            ss = {s: sb(f"ss_{s}", [P, NT]) for s in "ap"}
            lv = {s: sb(f"lv_{s}", [P, NT]) for s in "aprb"}
            y0 = {s: sb(f"y0_{s}", [P, NT]) for s in "aprb"}
            vv = {s: sb(f"vv_{s}", [P, NT]) for s in "aprb"}
            tt = {s: sb(f"tt_{s}", [P, NT]) for s in "aprb"}
            rs = {s: sb(f"rs_{s}", [P, NT]) for s in "aprb"}
            shift = {s: sb(f"shift_{s}", [P, NT]) for s in "rb"}
            st = {s: sb(f"st_{s}", [P, NT, 6]) for s in "rb"}
            mv = {s: sb(f"mv_{s}", [P, NT, 2]) for s in "rb"}
            lg = sb("lg", [P, NT, NE])
            pe_ = sb("pe_", [P, NT, NE])
            tmp8 = sb("tmp8", [P, NT, NE])
            oh = sb("oh", [P, NT, NE])
            ohb = sb("ohb", [P, NT, NE], BF16)
            filled = sb("filled", [P, NE])
            mx = sb("mx", [P, NT])
            sm = sb("sm", [P, NT])
            pm = sb("pm", [P, NT])
            wm = sb("wm", [P, NT])
            slot_f = sb("slot_f", [P, NT])
            over = sb("over", [P, NT])
            slot_i = sb("slot_i", [P, NT], U32)
            token = sb("token", [P, NT])

            dA = [bank(f"dA{i}") for i in range(3)]
            hB = [bank(f"hB{i}") for i in range(2)]
            aB = bank("aB")
            pB = [bank(f"pB{i}") for i in range(2)]

            names = """small_loaded gates_loaded dt_loaded late_loaded a_exp started tables_ready hidden_cleared zeroed zero_tile
                xa_loaded a_ss a_ln a_y0 a_newton a_rs xn_ready a_ready a_free g_clamped g_ln g_ready z_ready b_stored
                sp_exp sp_l sp_m sp_c sp_s dt_ready u_ready ub_ready da_ready scan_done carry_saved ht_ready stt_done
                xp_loaded p_ss p_ln p_y0 p_newton p_rs x1n_ready x1x_ready f_clamped f_ln f_sig ga_ready
                r_stats r_aggr r_ln r_y0 r_newton r_rs r_shift row_ready b_stats b_aggr b_ln b_y0 b_newton b_rs b_shift
                base_ready base_stored probs_ready rt_step oh_ready slot_ready scattered""".split()
            s = {n: sem(n) for n in names}
            p_ready = [sem(f"p_ready{i}") for i in range(2)]
            p_free = [sem(f"p_free{i}") for i in range(2)]
            b_loaded = [sem(f"b_loaded{i}") for i in range(4)]
            passed_sp, passed_pool, passed_act, passed_dve, passed_pe = (sem(f"passed_{e}") for e in ("sp", "pool", "act", "dve", "pe"))

            STAGES = {"norm": (-2, NCH - 3), "project": (-1, NCH - 2), "scan": (0, NCH - 1), "feed": (1, NCH), "route": (2, NCH + 1)}

            def on(stage, i):
                first, last = STAGES[stage]
                return not isinstance(i, int) or first <= i <= last

            def iterations(eng, iteration):
                for i in range(-2, 2):
                    iteration(i, i % 2)
                if NCH > 4:
                    with eng.Fori(0, (NCH - 4) // 2) as k:
                        iteration(k * 2 + 2, 0)
                        iteration(k * 2 + 3, 1)
                for i in range(NCH - 2, NCH + 2):
                    iteration(i, i % 2)

            at = STEPS

            def in_order(*jobs):
                return [(name, stage) for _, name, stage in sorted((step, name, stage) for step, name, stage in jobs)]

            A_RING = in_order(
                *((at["pe_xT"][j], f"xT{j}", "project") for j in range(2)),
                *((at["pe_gate_in"][j], f"{('gate', 'in')[j % 2]}{j // 2}", "project") for j in range(2 * DB)),
                (at["pe_bc"][0], "bc", "project"), *((at["pe_dt"][2 * d], f"dt{d}", "project") for d in range(DB)),
                (at["pe_bcT"], "bcT", "project"), *((at["pe_xlT"][j], f"xlT{j}", "route") for j in range(2)),
                (at["pe_logits"], "logits", "route"), (at["pe_counts"], "counts", "route"))
            P_RING = [in_order((b, f"acc{b}", "feed"), (b + 2, f"acc{b + 2}", "feed"), (at["pe_down"][4 * b], f"down{b}", "route"),
                               (at["pe_out"][2 * b], f"out{b}", "feed"), (at["pe_x1T"][b], f"x1T{b}", "feed"),
                               *((at["pe_gate_up"][2 * f + b], f"{('gate', 'up')[b]}{f}", "feed") for f in range(FB))) for b in range(2)]

            def before(ring, i, job=None):
                if not isinstance(i, int):
                    return i * len(ring) + (before(ring, 2, job) - 2 * len(ring))
                n = sum(on(stage, j) for j in range(-2, i) for _, stage in ring)
                for name, stage in ring:
                    if name == job or job is None:
                        break
                    n += on(stage, i)
                return n

            def a_count(i, job):
                return before(A_RING, i, job) + 1

            def p_count(b, i, job):
                return before(P_RING[b], i, job) + 1

            def dA_bank(k):
                return 1 if k == NS * DB - 1 else k % 3

            def dA_before(k):
                return next(j for j in range(k - 1, k - 5, -1) if dA_bank(j % (NS * DB)) == dA_bank(k))

            block = ctx.enter_context(nc.Block())

            @block.sync
            def _(sp):
                sp.dma_start(xa[:, :, :], chunk_rows(x_rows, 0)).then_inc(s["xa_loaded"], 16)
                for dst, src, done in (
                    (cst[:, :], consts, "small_loaded"), (norm1_s[:, :], norm1, "small_loaded"), (norm2_s[:, :], norm2, "small_loaded"),
                    (dt_b_s[:, :], dt_b, "small_loaded"), (dp_s[:, :], dp, "small_loaded"), (A[:, :, :], a_log, "small_loaded"),
                    (w_gate_s[:, :, :], w_gate.rearrange("(k p) e -> p k e", p=P), "gates_loaded"),
                    (w_in_s[:, :, :], w_in.rearrange("(k p) e -> p k e", p=P), "gates_loaded"),
                    (w_x_s[:, :, :], w_x.rearrange("(k p) e -> p k e", p=P), "dt_loaded"),
                    (w_dt_s[:, :, :], w_dt.rearrange("(k p) e -> p k e", p=P), "dt_loaded"),
                    (w_out_s[:, :, :], w_out.rearrange("(k p) e -> p k e", p=P), "late_loaded"),
                    (w_fg_s[:, :, :], w_fg.rearrange("(k p) e -> p k e", p=P), "late_loaded"),
                    (w_fu_s[:, :, :], w_fu.rearrange("(k p) e -> p k e", p=P), "late_loaded"),
                    (w_fd_s[:, 0:FB - 1, :], w_fd[0:P * (FB - 1), :].rearrange("(k p) e -> p k e", p=P), "late_loaded"),
                    (w_fd_s[0:FW[-1], FB - 1, :], w_fd[P * (FB - 1):FF, :], "late_loaded"),
                    (wg_s[:, :, :], wg.rearrange("(k p) e -> p k e", p=P), "late_loaded"),
                ):
                    sp.dma_start(dst, src).then_inc(s[done], 16)

                def iteration(i, par):
                    for n in range(NS):
                        if on("norm", i) and n == 1:
                            c = i + 2
                            if not isinstance(c, int) or c > 0:
                                if some(v := a_count(i, "xT1")):
                                    sp.wait_ge(s["a_ready"], v)
                                    sp.sem_inc(passed_sp, 1)
                                sp.dma_start(xa[:, :, :], chunk_rows(x_rows, c)).then_inc(s["xa_loaded"], 16)
                        if n % 2 == 0:
                            g, c, from_par = (n // 2 + 1, i, par) if n < NS - 2 else (0, i + 1, 1 - par)
                            if on("scan", c):
                                if g == 0:
                                    sp.wait_ge(s["b_stored"], (c + 1) * 16)
                                    sp.sem_inc(passed_sp, 1)
                                if some(v := c * NS + 2 * g - 6):
                                    sp.wait_ge(s["ub_ready"], v)
                                    sp.sem_inc(passed_sp, 1)
                                sp.dma_start(b_all[:, 2 * (g % 4):2 * (g % 4) + 2, :],
                                             b_scratch[from_par, 2 * g:2 * g + 2, :].partition_broadcast(P)).then_inc(b_loaded[g % 4], 16)
                        if first(i, NCH) and n == 0:
                            sp.wait_ge(s["ub_ready"], NCH * NS)
                            load_w1(sp, 0)
                            load_w2(sp, 0)
                        if on("feed", i) and n == 2:
                            c = i - 1
                            if some(v := c):
                                sp.wait_ge(s["x1x_ready"], v)
                                sp.sem_inc(passed_sp, 1)
                            sp.dma_start(xp[:, :, :], chunk_rows(x_rows, c)).then_inc(s["xp_loaded"], 16)
                        if on("project", i) and n == 9:
                            sp.wait_ge(s["a_free"], a_count(i, "bc"))
                            sp.sem_inc(passed_sp, 1)
                            if some(v := i * NS):
                                sp.wait_ge(s["ub_ready"], v)
                                sp.sem_inc(passed_sp, 1)
                            sp.dma_start(b_scratch[1 - par, :, :], bc[0:NS, :]).then_inc(s["b_stored"], 16)
                        if first(i, -1) and n == 12:
                            sp.wait_ge(s["zero_tile"], 2)
                            for g in range(S // T):
                                sp.dma_start(chunk_rows(slots_dram, g), row[:, :, :]).then_inc(s["zeroed"], 16)
                        if on("route", i) and n == NS - 1:
                            c = i - 2
                            sp.wait_ge(s["base_ready"], c + 1)
                            sp.sem_inc(passed_sp, 1)
                            sp.dma_start(chunk_rows(out_rows, c), base_out).then_inc(s["base_stored"], 16)

                iterations(sp, iteration)
                sp.wait_ge(s["base_stored"], 16 * NCH)
                sp.wait_ge(s["scattered"], 16 * NT * NCH)

            @block.gpsimd
            def _(pool):
                def iteration(i, par):
                    for n in range(NS):
                        if on("scan", i):
                            c = i
                            if n == 0:
                                pool.wait_ge(s["u_ready"], 2 * c + 2)
                            if n % 2 == 0:
                                pool.wait_ge(b_loaded[(n // 2) % 4], (2 * c + n // 8 + 1) * 16)
                            if some(v := 64 * c + 4 * (n - 1)):
                                pool.wait_ge(s["scan_done"], v)
                            pool.tensor_tensor(ub[n % 2][:, :, :], u[par][:, :, :],
                                               b_all[:, n % 8, :].unsqueeze(1).broadcast_to([P, DB, T]), ALU.mult).then_inc(s["ub_ready"], 1)
                        side(i, par, n)

                def gate_up(c, g):
                    pool.wait_ge(s["f_sig"], 3 * c + g + 1)
                    pool.wait_ge(p_free[1], p_count(1, c + 1, f"up{2 * g + 1}"))
                    pool.tensor_tensor(gu[:, 2 * g:2 * g + 2, :], gu[:, 2 * g:2 * g + 2, :], fe[g % 2][:, :, :], ALU.mult).then_inc(s["ga_ready"], 1)

                def side(i, par, n):
                    if on("route", i) and n in (0, 1):
                        gate_up(i - 2, n + 1)
                    if on("project", i):
                        c, q = i + 1, 1 - par
                        for half in range(2):
                            d = slice(2 * half, 2 * half + 2)
                            if n == at["pool_z"][half]:
                                pool.wait_ge(s["g_ready"], 2 * c + half + 1)
                                pool.wait_ge(s["a_free"], a_count(i, f"in{2 * half + 1}"))
                                pool.tensor_tensor(z[q][:, d, :], z[q][:, d, :], u[q][:, d, :], ALU.mult).then_inc(s["z_ready"], 1)
                            if n == at["pool_lost"][half]:
                                pool.wait_ge(s["sp_m"], 2 * c + half + 1)
                                pool.tensor_tensor(sp_fix, u[q][:, d, :], sp_fix, ALU.subtract).then_inc(s["sp_c"], 1)
                            if n == at["pool_sum"][half]:
                                pool.wait_ge(s["sp_c"], 2 * c + half + 1)
                                pool.wait_ge(s["sp_l"], 2 * c + half + 1)
                                pool.tensor_tensor(sp_fix, sp_fix, sp_log, ALU.add).then_inc(s["sp_s"], 1)
                            if n == at["pool_u"][half]:
                                pool.wait_ge(s["dt_ready"], 2 * c + half + 1)
                                pool.tensor_tensor(u[q][:, d, :], dt[q][:, d, :], z[q][:, d, :], ALU.mult).then_inc(s["u_ready"], 1)
                    if on("feed", i):
                        c = i - 1
                        if n == at["pool_x1x"]:
                            pool.wait_ge(s["xp_loaded"], 16 * (c + 1))
                            pool.wait_ge(s["x1n_ready"], c + 1)
                            pool.tensor_tensor(x1[:, :, :], x1[:, :, :], xp[:, :, :], ALU.add).then_inc(s["x1x_ready"], 1)
                        if n == at["pool_ga0"]:
                            gate_up(c, 0)
                    if on("route", i) and n == at["pool_scatter"]:
                        c = i - 2
                        pool.wait_ge(s["slot_ready"], c + 1)
                        pool.sem_inc(passed_pool, 1)
                        pool.wait_ge(s["zeroed"], 16 * (S // T))
                        for t in range(NT):
                            pool.indirect_dma_start(out=slots_dram, out_offset=bass.IndirectOffsetOnAxis(slot_i[:, t:t + 1], 0),
                                                    in_=row[:, t, :], in_offset=None, bounds_check=S - 1,
                                                    oob_is_err=False).then_inc(s["scattered"], 16)

                iterations(pool, iteration)

            @block.scalar
            def _(act):
                act.preload_act_table_set(EXP_LN)
                act.wait_ge(s["small_loaded"], 6 * 16)
                act.activation(A[:, :, :], A[:, :, :], ACT.Exp).then_inc(s["a_exp"], 1)
                act.wait_ge(s["started"], 1)

                def start_rsqrt(src, scale, eps, side, ln_done, y0_done, count):
                    act.activation(lv[side][:, :], src, ACT.Ln, bias=eps[:, 0:1], scale=scale).then_inc(s[ln_done], 1)
                    act.wait_ge(s[ln_done], count)
                    act.activation(y0[side][:, :], lv[side][:, :], ACT.Exp, scale=-0.5).then_inc(s[y0_done], 1)

                def iteration(i, par):
                    for k in range(NS * DB):
                        if on("scan", i):
                            n, db = k // DB, k % DB
                            if k == 0:
                                act.wait_ge(s["dt_ready"], 2 * i + 2)
                            if some(v := 64 * i + (dA_before(k) + 1)):
                                act.wait_ge(s["scan_done"], v)
                            act.activation(dA[dA_bank(k)][:, :], dt[par][:, db, :], ACT.Exp, scale=A[:, db, n:n + 1]).then_inc(s["da_ready"], 1)
                            if 0 <= k - at["act_first_fold"] < NT:
                                first_fold(i, par, k - at["act_first_fold"])
                            if k >= DB + at["act_save"] and k % DB == at["act_save"]:
                                save(i, k // DB - 1)
                        if on("norm", i):
                            norm(i, k)
                        if on("project", i):
                            project(i, 1 - par, k)
                        if on("feed", i):
                            feed(i, k)
                        if on("route", i):
                            route(i, k)

                    if on("scan", i):
                        save(i, NS - 1)

                def first_fold(i, par, t):
                    if t == 0:
                        act.wait_ge(s["a_free"], before(A_RING, i))
                    act.wait_ge(s["ht_ready"], 64 * i + (t + 1))
                    act.activation(acc[:, t, :], hB[t % 2][:, :], ACT.Copy, scale=c_tok[par][:, t, 0:1]).then_inc(s["stt_done"], 1)

                def save(i, n):
                    act.wait_ge(s["scan_done"], 64 * i + 4 * n + 4)
                    act.sem_inc(passed_act, 1)
                    act.activation(carry[:, n * DB:(n + 1) * DB], h[n % 2][:, :, T - 1], ACT.Copy,
                                   scale=cst[:, bass.ds(i + (columns["keep"][0] + 1), 1)]).then_inc(s["carry_saved"], 1)

                def norm(i, k):
                    c = i + 2
                    if k == at["act_ss"]:
                        act.wait_ge(s["xa_loaded"], 16 * (c + 1))
                        if some(v := before(A_RING, i, "bc")):
                            act.wait_ge(s["a_ready"], v)
                        for t in range(NT):
                            last = act.activation(hT[:, t // 2, (t % 2) * D:(t % 2 + 1) * D], xa[:, t, :], ACT.Square, accum_out=ss["a"][:, t:t + 1])
                        last.then_inc(s["a_ss"], 1)
                        act.wait_ge(s["a_ss"], c + 1)
                        start_rsqrt(ss["a"][:, :], 1.0 / D, eps_rms, "a", "a_ln", "a_y0", c + 1)
                    if k == at["act_xn"]:
                        act.wait_ge(s["a_rs"], c + 1)
                        for t in range(NT):
                            last = act.activation(xa[:, t, :], xa[:, t, :], ACT.Copy, scale=rs["a"][:, t:t + 1])
                        last.then_inc(s["xn_ready"], 1)

                def project(i, q, k):
                    c = i + 1
                    if k in at["act_hT"]:
                        j = at["act_hT"].index(k)
                        act.wait_ge(s["a_ready"], a_count(i, f"xT{j}"))
                        act.activation(hT[:, j, :], aB[:, :], ACT.Copy, scale=norm1_s[:, j:j + 1]).then_inc(s["a_free"], 1)
                    if k in at["act_gate_in"]:
                        d, kind = divmod(at["act_gate_in"].index(k), 2)
                        if kind == 0:
                            if d == 0 and some(v := 16 * i):
                                act.wait_ge(s["ub_ready"], v)
                            act.wait_ge(s["a_ready"], a_count(i, f"gate{d}"))
                            act.activation(u[q][:, d, :], aB[:, :], ACT.Exp, scale=-1.0).then_inc(s["a_free"], 1)
                        else:
                            if on("feed", i) and d == 0:
                                act.wait_ge(p_free[0], p_count(0, i, "acc2"))
                                act.wait_ge(p_free[1], p_count(1, i, "acc3"))
                            act.wait_ge(s["a_ready"], a_count(i, f"in{d}"))
                            act.activation(z[q][:, d, :], aB[:, :], ACT.Copy).then_inc(s["a_free"], 1)
                    if k in at["act_sigmoid"]:
                        half = at["act_sigmoid"].index(k)
                        d = slice(2 * half, 2 * half + 2)
                        act.wait_ge(s["g_clamped"], 2 * c + half + 1)
                        act.activation(u[q][:, d, :], u[q][:, d, :], ACT.Ln, bias=1.0).then_inc(s["g_ln"], 1)
                        act.wait_ge(s["g_ln"], 2 * c + half + 1)
                        act.activation(u[q][:, d, :], u[q][:, d, :], ACT.Exp, scale=-1.0).then_inc(s["g_ready"], 1)
                    if k == at["act_bc"]:
                        act.wait_ge(s["a_ready"], a_count(i, "bc"))
                        if some(v := 16 * c):
                            act.wait_ge(s["b_stored"], v)
                        act.activation(bc[:, :], aB[0:2 * NS, :], ACT.Copy).then_inc(s["a_free"], 1)
                    if k in at["act_dt"]:
                        d = at["act_dt"].index(k)
                        act.wait_ge(s["z_ready"], 2 * c + 2)
                        act.wait_ge(s["a_ready"], a_count(i, f"dt{d}"))
                        act.activation(dt[q][:, d, :], aB[:, :], ACT.Relu, bias=dt_b_s[:, d:d + 1])
                        act.activation(u[q][:, d, :], aB[:, :], ACT.Abs, bias=dt_b_s[:, d:d + 1]).then_inc(s["a_free"], 1)
                    for half in range(2):
                        dd = slice(2 * half, 2 * half + 2)
                        if k == at["act_e"][half]:
                            act.wait_ge(s["a_free"], a_count(i, f"dt{2 * half + 1}"))
                            act.activation(u[q][:, dd, :], u[q][:, dd, :], ACT.Exp, scale=-1.0).then_inc(s["sp_exp"], 1)
                        if k == at["act_ln"][half]:
                            act.wait_ge(s["sp_exp"], 2 * c + half + 1)
                            if half == 1:
                                act.wait_ge(s["sp_s"], 2 * c + 1)
                            elif on("feed", i):
                                act.wait_ge(p_ready[0], p_count(0, i, "x1T0"))
                                act.wait_ge(p_ready[1], p_count(1, i, "x1T1"))
                            else:
                                if some(v := 2 * c):
                                    act.wait_ge(s["sp_s"], v)
                            act.activation(sp_log, u[q][:, dd, :], ACT.Ln, bias=1.0).then_inc(s["sp_l"], 1)
                    if k == at["act_c_tok"]:
                        act.wait_ge(s["a_ready"], a_count(i, "bcT"))
                        act.activation(c_tok[q][:, :, :], aB[:, 0:NT * 2 * NS].rearrange("p (t m) -> p t m", m=2 * NS)[:, :, NS:2 * NS],
                                       ACT.Copy).then_inc(s["a_free"], 1)

                def feed(i, k):
                    c = i - 1
                    if k == at["act_p_ss"]:
                        act.wait_ge(p_free[0], p_count(0, i, "out0"))
                        act.wait_ge(p_free[1], p_count(1, i, "out1"))
                        for t in range(NT):
                            last = act.activation(x1n[:, t, :], x1[:, t, :], ACT.Square, accum_out=ss["p"][:, t:t + 1])
                        last.then_inc(s["p_ss"], 1)
                        act.wait_ge(s["p_ss"], c + 1)
                        start_rsqrt(ss["p"][:, :], 1.0 / D, eps_rms, "p", "p_ln", "p_y0", c + 1)
                    if k == at["act_x1n"]:
                        act.wait_ge(s["p_rs"], c + 1)
                        for t in range(NT):
                            last = act.activation(x1n[:, t, :], x1[:, t, :], ACT.Copy, scale=rs["p"][:, t:t + 1])
                        last.then_inc(s["x1n_ready"], 1)
                    if k in at["act_hnT"]:
                        j = at["act_hnT"].index(k)
                        act.wait_ge(p_ready[j], p_count(j, i, f"x1T{j}"))
                        act.activation(hnT[:, j, :], pB[j][:, :], ACT.Copy, scale=norm2_s[:, j:j + 1]).then_inc(p_free[j], 1)
                    if k in at["act_gate"]:
                        f = at["act_gate"].index(k)
                        w = FW[f]
                        act.wait_ge(p_ready[0], p_count(0, i, f"gate{f}"))
                        if f % 2 == 0 and some(v := 3 * c + f // 2 - 1):
                            act.wait_ge(s["ga_ready"], v)
                        if f == 0 and first(c, 0):
                            act.wait_ge(s["hidden_cleared"], 1)
                        if f == 0 and on("route", i):
                            act.wait_ge(p_ready[1], p_count(1, i, "down1"))
                        act.activation(fe[(f // 2) % 2][0:w, f % 2, :], pB[0][0:w, :], ACT.Exp, scale=-1.0)
                        act.activation(gu[0:w, f, :], pB[0][0:w, :], ACT.Copy).then_inc(p_free[0], 1)
                    if k in at["act_ffn_sigmoid"]:
                        g = at["act_ffn_sigmoid"].index(k)
                        act.wait_ge(s["f_clamped"], 3 * c + g + 1)
                        act.activation(fe[g % 2][:, :, :], fe[g % 2][:, :, :], ACT.Ln, bias=1.0).then_inc(s["f_ln"], 1)
                        act.wait_ge(s["f_ln"], 3 * c + g + 1)
                        act.activation(fe[g % 2][:, :, :], fe[g % 2][:, :, :], ACT.Exp, scale=-1.0).then_inc(s["f_sig"], 1)

                def route(i, k):
                    c = i - 2
                    if k == at["act_r_rsqrt"]:
                        act.wait_ge(s["r_aggr"], c + 1)
                        start_rsqrt(mv["r"][:, :, 1], 1.0, eps_ln, "r", "r_ln", "r_y0", c + 1)
                    if k == at["act_row"]:
                        act.wait_ge(s["r_rs"], c + 1)
                        act.wait_ge(s["r_shift"], c + 1)
                        for t in range(NT):
                            last = act.activation(row[:, t, 0:D], row[:, t, 0:D], ACT.Identity, scale=rs["r"][:, t:t + 1], bias=shift["r"][:, t:t + 1])
                        last.then_inc(s["row_ready"], 1)
                    if k in at["act_xlT"]:
                        j = at["act_xlT"].index(k)
                        act.wait_ge(s["a_ready"], a_count(i, f"xlT{j}"))
                        if some(v := 16 * c):
                            act.wait_ge(s["base_stored"], v)
                        act.activation(xlT[:, j, :], aB[:, :], ACT.Copy).then_inc(s["a_free"], 1)
                    if k == at["act_probs"]:
                        act.wait_ge(s["a_free"], a_count(i, "logits"))
                        act.activation(pe_[:, :, :], lg[:, :, :], ACT.Exp).then_inc(s["probs_ready"], 1)
                    if k == at["act_b_rsqrt"]:
                        act.wait_ge(s["b_aggr"], c + 1)
                        start_rsqrt(mv["b"][:, :, 1], 1.0, eps_ln, "b", "b_ln", "b_y0", c + 1)
                    if k == at["act_base"]:
                        act.wait_ge(s["b_rs"], c + 1)
                        act.wait_ge(s["b_shift"], c + 1)
                        act.wait_ge(s["a_ready"], a_count(i, "logits"))
                        for t in range(NT):
                            last = act.activation(base_out[:, t, :], row[:, t, 0:D], ACT.Identity, scale=rs["b"][:, t:t + 1], bias=shift["b"][:, t:t + 1])
                        last.then_inc(s["base_ready"], 1)

                iterations(act, iteration)

            @block.vector
            def _(dve):
                dve.memset(eps_rms[:, :], RMS_EPS)
                dve.memset(eps_ln[:, :], LN_EPS)
                dve.memset(carry[:, :], 0.0)
                dve.wait_ge(s["a_exp"], 1)
                dve.tensor_scalar(A[:, :, :], A[:, :, :], -1.0, None, ALU.mult).then_inc(s["started"], 1)
                dve.memset(row[:, :, :], 0.0).then_inc(s["zero_tile"], 1)
                dve.wait_ge(s["zero_tile"], 1)
                dve.tensor_scalar(row_index[:, :, D + 1], row[:, :, D + 1], 1.0, NOWHERE, ALU.mult, ALU.add).then_inc(s["zero_tile"], 1)
                dve.tensor_copy(ones_b[:, :], cst[:, columns["ones"][0]:columns["ones"][1]])
                dve.tensor_copy(earlier_b[:, :], cst[:, columns["earlier"][0]:columns["earlier"][1]])
                dve.tensor_copy(filled[:, :], cst[:, columns["base"][0]:columns["base"][1]])
                dve.tensor_copy(token[:, :], cst[:, columns["token"][0]:columns["token"][1]]).then_inc(s["tables_ready"], 1)
                dve.wait_ge(s["tables_ready"], 1)

                def clear_hidden():
                    dve.memset(gu[:, :, :], 0.0)
                    dve.memset(fe[0][:, :, :], 0.0)
                    dve.memset(fe[1][:, :, :], 0.0).then_inc(s["hidden_cleared"], 1)

                def newton(src, scale, eps, side, y0_done, step, done, c):
                    dve.wait_ge(s[y0_done], c + 1)
                    dve.tensor_scalar(vv[side][:, :], src, scale, eps, ALU.mult, ALU.add)
                    dve.tensor_tensor(tt[side][:, :], y0[side][:, :], y0[side][:, :], ALU.mult).then_inc(s[step], 1)
                    dve.wait_ge(s[step], 3 * c + 1)
                    dve.tensor_tensor(tt[side][:, :], tt[side][:, :], vv[side][:, :], ALU.mult).then_inc(s[step], 1)
                    dve.wait_ge(s[step], 3 * c + 2)
                    dve.tensor_scalar(tt[side][:, :], tt[side][:, :], -0.5, 1.5, ALU.mult, ALU.add).then_inc(s[step], 1)
                    dve.wait_ge(s[step], 3 * c + 3)
                    dve.tensor_tensor(rs[side][:, :], y0[side][:, :], tt[side][:, :], ALU.mult).then_inc(s[done], 1)

                def shifts(side, done, shifted, c):
                    dve.wait_ge(s[done], c + 1)
                    dve.scalar_tensor_tensor(out=shift[side][:, :], in0=mv[side][:, :, 0], scalar=-1.0, in1=rs[side][:, :],
                                             op0=ALU.mult, op1=ALU.mult).then_inc(s[shifted], 1)

                def iteration(i, par):
                    def fold(n, t):
                        dve.wait_ge(s["ht_ready"], 64 * i + 4 * n + t + 1)
                        dve.wait_ge(s["stt_done"], 64 * i + (4 if n == 1 else 4 * (n - 1) + t + 1))
                        dve.scalar_tensor_tensor(out=acc[:, t, :], in0=hB[t % 2][:, :], scalar=c_tok[par][:, t, n:n + 1], in1=acc[:, t, :],
                                                 op0=ALU.mult, op1=ALU.add).then_inc(s["stt_done"], 1)

                    for k in range(NS * DB):
                        if on("scan", i):
                            n, db = k // DB, k % DB
                            if k == 0:
                                dve.wait_ge(s["a_free"], before(A_RING, i))
                            if db == 0:
                                dve.wait_ge(s["ub_ready"], i * NS + n + 1)
                                if some(v := 64 * i + 4 * (n - 1)):
                                    dve.wait_ge(s["ht_ready"], v)
                                if some(v := i * NS + n - 1):
                                    dve.wait_ge(s["carry_saved"], v)
                            dve.wait_ge(s["da_ready"], 64 * i + k + 1)
                            dve.tensor_tensor_scan(h[n % 2][:, db, :], dA[dA_bank(k)][:, :], ub[n % 2][:, db, :],
                                                   carry[:, k:k + 1], ALU.mult, ALU.add).then_inc(s["scan_done"], 1)
                            if n > 1:
                                fold(n - 1, db)
                        if first(i, 0) and k == 0:
                            clear_hidden()
                        if on("norm", i) and k == at["dve_a_newton"]:
                            newton(ss["a"][:, :], 1.0 / D, RMS_EPS, "a", "a_y0", "a_newton", "a_rs", i + 2)
                        if on("project", i):
                            project(i, 1 - par, k)
                        if on("feed", i):
                            feed(i, par, k)
                        if on("route", i):
                            route(i, k)
                    if on("scan", i):
                        for t in range(NT):
                            fold(NS - 1, t)

                def project(i, q, k):
                    c = i + 1
                    for half in range(2):
                        d = slice(2 * half, 2 * half + 2)
                        if k == at["dve_cap"][half]:
                            dve.wait_ge(s["a_free"], a_count(i, f"gate{2 * half + 1}"))
                            dve.tensor_scalar(u[q][:, d, :], u[q][:, d, :], EXP_CAP, None, ALU.min).then_inc(s["g_clamped"], 1)
                        if k == at["dve_rounded"][half]:
                            dve.wait_ge(s["sp_exp"], 2 * c + half + 1)
                            if half == 1:
                                dve.wait_ge(s["dt_ready"], 2 * c + 1)
                            elif on("feed", i):
                                dve.wait_ge(p_ready[1], p_count(1, i, "out1"))
                            dve.tensor_scalar(sp_fix, u[q][:, d, :], 1.0, -1.0, ALU.add, ALU.add).then_inc(s["sp_m"], 1)
                        if k == at["dve_dt"][half]:
                            dve.wait_ge(s["sp_s"], 2 * c + half + 1)
                            dve.wait_ge(s["a_free"], a_count(i, f"dt{2 * half + 1}"))
                            dve.tensor_tensor(dt[q][:, d, :], dt[q][:, d, :], sp_fix, ALU.add).then_inc(s["dt_ready"], 1)

                def feed(i, par, k):
                    c = i - 1
                    if k < DB:
                        if k == 0 and on("project", i - 1):
                            dve.wait_ge(s["dt_ready"], 2 * i + 2)
                        dve.wait_ge(p_ready[k % 2], p_count(k % 2, i, f"acc{k}"))
                        dve.scalar_tensor_tensor(out=yT[:, k, :], in0=z[1 - par][:, k, :], scalar=dp_s[:, k:k + 1],
                                                 in1=pB[k % 2][:, :], op0=ALU.mult, op1=ALU.add).then_inc(p_free[k % 2], 1)
                    if k in at["dve_x1"]:
                        b = at["dve_x1"].index(k)
                        dve.wait_ge(s["xp_loaded"], 16 * (c + 1))
                        dve.wait_ge(p_ready[b], p_count(b, i, f"out{b}"))
                        dve.tensor_tensor(x1[:, 2 * b:2 * b + 2, :], pB[b][:, :].rearrange("p (t d) -> p t d", d=D),
                                          xp[:, 2 * b:2 * b + 2, :], ALU.add).then_inc(p_free[b], 1)
                    if k == at["dve_p_newton"]:
                        newton(ss["p"][:, :], 1.0 / D, RMS_EPS, "p", "p_y0", "p_newton", "p_rs", c)
                    if k in at["dve_gate_up"]:
                        f = at["dve_gate_up"].index(k)
                        w = FW[f]
                        dve.wait_ge(p_free[0], p_count(0, i, f"gate{f}"))
                        dve.wait_ge(p_ready[1], p_count(1, i, f"up{f}"))
                        dve.tensor_tensor(gu[0:w, f, :], pB[1][0:w, :], gu[0:w, f, :], ALU.mult).then_inc(p_free[1], 1)
                    if k in at["dve_ffn_cap"]:
                        g = at["dve_ffn_cap"].index(k)
                        dve.wait_ge(p_free[0], p_count(0, i, f"gate{2 * g + 1}"))
                        dve.tensor_scalar(fe[g % 2][:, :, :], fe[g % 2][:, :, :], EXP_CAP, None, ALU.min).then_inc(s["f_clamped"], 1)

                def route(i, k):
                    c = i - 2
                    if k in at["dve_row"]:
                        b = at["dve_row"].index(k)
                        if b == 0:
                            if first(c, 0):
                                dve.wait_ge(s["zeroed"], 16 * (S // T))
                            if some(v := 64 * c):
                                dve.wait_ge(s["scattered"], v)
                            dve.wait_ge(s["x1x_ready"], c + 1)
                        dve.wait_ge(p_ready[b], p_count(b, i, f"down{b}"))
                        dve.tensor_tensor(row[:, 2 * b:2 * b + 2, 0:D], pB[b][:, :].rearrange("p (t d) -> p t d", d=D),
                                          x1[:, 2 * b:2 * b + 2, :], ALU.add).then_inc(p_free[b], 1)
                    if k == at["dve_r_stats"]:
                        dve.wait_ge(p_free[0], p_count(0, i, "down0"))
                        dve.wait_ge(p_free[1], p_count(1, i, "down1"))
                        for t in range(NT):
                            last = dve.bn_stats(st["r"][:, t, :], row[:, t, 0:D])
                        last.then_inc(s["r_stats"], 1)
                    if k == at["dve_r_aggr"]:
                        dve.wait_ge(s["r_stats"], c + 1)
                        dve.sem_inc(passed_dve, 1)
                        for t in range(NT):
                            last = dve.bn_aggr(mv["r"][:, t, :], st["r"][:, t, :])
                        last.then_inc(s["r_aggr"], 1)
                    if k == at["dve_r_newton"]:
                        newton(mv["r"][:, :, 1], 1.0, LN_EPS, "r", "r_y0", "r_newton", "r_rs", c)
                        shifts("r", "r_rs", "r_shift", c)
                    if k == at["dve_logits"]:
                        dve.wait_ge(s["a_ready"], a_count(i, "logits"))
                        logits = aB[:, 0:NT * NE].rearrange("p (t e) -> p t e", e=NE)
                        dve.tensor_reduce(mx[:, :], logits, AX.X, ALU.max).then_inc(s["rt_step"], 1)
                        dve.wait_ge(s["rt_step"], 9 * c + 1)
                        dve.tensor_tensor(lg[:, :, :], logits, mx[:, :].unsqueeze(2).broadcast_to([P, NT, NE]), ALU.subtract).then_inc(s["a_free"], 1)
                    if k == at["dve_b_stats"]:
                        dve.wait_ge(s["row_ready"], c + 1)
                        for t in range(NT):
                            last = dve.bn_stats(st["b"][:, t, :], row[:, t, 0:D])
                        last.then_inc(s["b_stats"], 1)
                    if k == at["dve_b_aggr"]:
                        dve.wait_ge(s["b_stats"], c + 1)
                        dve.sem_inc(passed_dve, 1)
                        for t in range(NT):
                            last = dve.bn_aggr(mv["b"][:, t, :], st["b"][:, t, :])
                        last.then_inc(s["b_aggr"], 1)
                    if k == at["dve_choice"]:
                        dve.wait_ge(s["probs_ready"], c + 1)
                        dve.tensor_reduce(sm[:, :], pe_[:, :, :], AX.X, ALU.add)
                        dve.tensor_reduce(pm[:, :], pe_[:, :, :], AX.X, ALU.max).then_inc(s["rt_step"], 1)
                        dve.wait_ge(s["rt_step"], 9 * c + 2)
                        dve.tensor_tensor(tmp8[:, :, :], pe_[:, :, :], pm[:, :].unsqueeze(2).broadcast_to([P, NT, NE]), ALU.is_ge).then_inc(s["rt_step"], 1)
                        dve.reciprocal(sm[:, :], sm[:, :])
                        dve.wait_ge(s["rt_step"], 9 * c + 3)
                        dve.tensor_tensor(tmp8[:, :, :], tmp8[:, :, :], rank.unsqueeze(1).broadcast_to([P, NT, NE]), ALU.mult).then_inc(s["rt_step"], 1)
                        dve.wait_ge(s["rt_step"], 9 * c + 4)
                        dve.tensor_reduce(wm[:, :], tmp8[:, :, :], AX.X, ALU.max).then_inc(s["rt_step"], 1)
                        dve.wait_ge(s["rt_step"], 9 * c + 5)
                        dve.tensor_tensor(row[:, :, D], sm[:, :], pm[:, :], ALU.mult)
                        dve.tensor_tensor(oh[:, :, :], tmp8[:, :, :], wm[:, :].unsqueeze(2).broadcast_to([P, NT, NE]), ALU.is_equal).then_inc(s["rt_step"], 1)
                        dve.wait_ge(s["rt_step"], 9 * c + 6)
                        dve.tensor_copy(ohb[:, :, :], oh[:, :, :]).then_inc(s["oh_ready"], 1)
                        dve.tensor_copy(row_index[:, :, D + 1], token[:, :]).then_inc(s["rt_step"], 1)
                        dve.wait_ge(s["rt_step"], 9 * c + 7)
                        dve.tensor_scalar(token[:, :], token[:, :], float(T), None, ALU.add)
                    if k == at["dve_slot"]:
                        dve.wait_ge(s["a_ready"], a_count(i, "counts"))
                        counts = aB[:, 0:NT * NE].rearrange("p (t e) -> p t e", e=NE)
                        dve.tensor_tensor(tmp8[:, :, :], counts, filled[:, :].unsqueeze(1).broadcast_to([P, NT, NE]), ALU.add).then_inc(s["rt_step"], 1)
                        dve.wait_ge(s["rt_step"], 9 * c + 8)
                        dve.tensor_tensor(filled[:, :], filled[:, :], aB[:, NT * NE:NT * NE + NE], ALU.add).then_inc(s["a_free"], 1)
                        dve.tensor_tensor(tmp8[:, :, :], tmp8[:, :, :], oh[:, :, :], ALU.mult).then_inc(s["rt_step"], 1)
                        dve.wait_ge(s["rt_step"], 9 * c + 9)
                        dve.tensor_reduce(slot_f[:, :], tmp8[:, :, :], AX.X, ALU.add).then_inc(s["oh_ready"], 1)
                        dve.wait_ge(s["oh_ready"], 5 * c + 2)
                        dve.scalar_tensor_tensor(out=over[:, :], in0=wm[:, :], scalar=float(C), in1=slot_f[:, :], op0=ALU.mult, op1=ALU.add).then_inc(s["oh_ready"], 1)
                        dve.wait_ge(s["oh_ready"], 5 * c + 3)
                        dve.tensor_scalar(over[:, :], over[:, :], float(C * (NE + 1)), NOWHERE, ALU.is_ge, ALU.mult).then_inc(s["oh_ready"], 1)
                        dve.wait_ge(s["oh_ready"], 5 * c + 4)
                        dve.tensor_tensor(slot_f[:, :], slot_f[:, :], over[:, :], ALU.add).then_inc(s["oh_ready"], 1)
                        dve.wait_ge(s["oh_ready"], 5 * c + 5)
                        dve.tensor_copy(slot_i[:, :], slot_f[:, :]).then_inc(s["slot_ready"], 1)
                    if k == at["dve_b_newton"]:
                        newton(mv["b"][:, :, 1], 1.0, LN_EPS, "b", "b_y0", "b_newton", "b_rs", c)
                        shifts("b", "b_rs", "b_shift", c)

                iterations(dve, iteration)

            @block.tensor
            def _(pe):
                pe.wait_ge(s["small_loaded"], 6 * 16)
                pe.wait_ge(s["started"], 1)
                pe.wait_ge(s["gates_loaded"], 2 * 16)

                def transposes(to, tiles, done, rows=P):
                    for k, tile in enumerate(tiles):
                        last = pe.matmul(to[:, k * rows:(k + 1) * rows], tile, ident[0:rows, 0:rows], start=True, stop=True, is_transpose=True)
                    last.then_inc(done, 1)

                def product(to, pairs, steps, of, done=None):
                    for k, (lhsT, rhs) in zip(steps, pairs):
                        last = pe.matmul(to, lhsT, rhs, start=(k == 0), stop=(k == of - 1))
                    if done is not None:
                        last.then_inc(done, 1)

                def iteration(i, par):
                    def turn(n, t):
                        if t == 0:
                            pe.wait_ge(s["scan_done"], 64 * i + 4 * n + 4)
                        if some(v := 64 * i + 4 * n + t - 1):
                            pe.wait_ge(s["stt_done"], v)
                        transposes(hB[t % 2], [h[n % 2][:, db, t * P:(t + 1) * P] for db in range(DB)], s["ht_ready"])

                    for k in range(NS * DB):
                        if on("feed", i):
                            feed(i, k)
                        if on("project", i):
                            project(i, 1 - par, k)
                        if on("route", i):
                            route(i, k)
                        if on("scan", i) and k >= DB:
                            turn(k // DB - 1, k % DB)
                    if on("scan", i):
                        for t in range(NT):
                            turn(NS - 1, t)

                def project(i, q, k):
                    c = i + 1
                    if k in at["pe_xT"]:
                        j = at["pe_xT"].index(k)
                        pe.wait_ge(s["xn_ready"], c + 1)
                        if some(v := before(A_RING, i, f"xT{j}")):
                            pe.wait_ge(s["a_free"], v)
                        transposes(aB, [xa[:, t, j * P:(j + 1) * P] for t in range(NT)], s["a_ready"])
                    if k in at["pe_gate_in"]:
                        d, kind = divmod(at["pe_gate_in"].index(k), 2)
                        name, w = (("gate", w_gate_s), ("in", w_in_s))[kind]
                        pe.wait_ge(s["a_free"], before(A_RING, i, f"{name}{d}"))
                        product(aB[:, :], [(w[:, j, d * P:(d + 1) * P], hT[:, j, :]) for j in range(KD)], range(KD), KD, s["a_ready"])
                    if k in at["pe_bc"]:
                        j = 2 * at["pe_bc"].index(k)
                        if j == 0:
                            if first(c, 0):
                                pe.wait_ge(s["dt_loaded"], 2 * 16)
                            pe.wait_ge(s["a_free"], before(A_RING, i, "bc"))
                        pe.wait_ge(s["z_ready"], 2 * c + 1 + j // 2)
                        product(aB[0:2 * NS, :], [(w_x_s[:, m, :], z[q][:, m, :]) for m in (j, j + 1)], (j, j + 1), DB, s["a_ready"] if j else None)
                    if k in at["pe_dt"]:
                        d, j = divmod(2 * at["pe_dt"].index(k), DB)
                        if j == 0:
                            pe.wait_ge(s["a_free"], before(A_RING, i, f"dt{d}"))
                        product(aB[:, :], [(w_dt_s[:, m, d * P:(d + 1) * P], z[q][:, m, :]) for m in (j, j + 1)], (j, j + 1), DB,
                                s["a_ready"] if j else None)
                    if k == at["pe_bcT"]:
                        pe.wait_ge(s["a_free"], before(A_RING, i, "bcT"))
                        pe.sem_inc(passed_pe, 1)
                        transposes(aB, [bc[:, t * P:(t + 1) * P] for t in range(NT)], s["a_ready"], 2 * NS)

                def feed(i, k):
                    c = i - 1
                    if k < DB:
                        if k == 0:
                            pe.wait_ge(s["stt_done"], 64 * (c + 1))
                        if some(v := before(P_RING[k % 2], i, f"acc{k}")):
                            pe.wait_ge(p_free[k % 2], v)
                        transposes(pB[k % 2], [acc[:, t, k * P:(k + 1) * P] for t in range(NT)], p_ready[k % 2])
                    if k in at["pe_out"]:
                        t = at["pe_out"].index(k)
                        b = t // 2
                        if t == 0:
                            if first(c, 0):
                                pe.wait_ge(s["late_loaded"], 6 * 16)
                            pe.wait_ge(p_free[1], p_count(1, i, "acc3"))
                        if t % 2 == 0:
                            pe.wait_ge(p_free[b], before(P_RING[b], i, f"out{b}"))
                        product(pB[b][:, (t % 2) * D:(t % 2 + 1) * D], [(yT[:, j, t * P:(t + 1) * P], w_out_s[:, j, :]) for j in range(DB)],
                                range(DB), DB, p_ready[b] if t % 2 else None)
                    if k in at["pe_x1T"]:
                        j = at["pe_x1T"].index(k)
                        pe.wait_ge(s["x1n_ready"], c + 1)
                        pe.wait_ge(p_free[j], before(P_RING[j], i, f"x1T{j}"))
                        transposes(pB[j], [x1n[:, t, j * P:(j + 1) * P] for t in range(NT)], p_ready[j])
                    if k in at["pe_gate_up"]:
                        f, up = at["pe_gate_up"].index(k) // 2, at["pe_gate_up"].index(k) % 2
                        if k == at["pe_gate_up"][0]:
                            pe.wait_ge(p_free[1], p_count(1, i, "x1T1"))
                        pe.wait_ge(p_free[up], before(P_RING[up], i, f"{('gate', 'up')[up]}{f}"))
                        w = w_fu_s if up else w_fg_s
                        product(pB[up][0:FW[f], :], [(w[:, j, f * P:f * P + FW[f]], hnT[:, j, :]) for j in range(KD)], range(KD), KD, p_ready[up])

                def route(i, k):
                    c = i - 2
                    if k in at["pe_down"]:
                        n = at["pe_down"].index(k)
                        t, later = n // 2, n % 2
                        b = t // 2
                        if n < 2:
                            pe.wait_ge(s["ga_ready"], 3 * c + 2 + later)
                        if n % 4 == 0:
                            pe.wait_ge(p_free[b], before(P_RING[b], i, f"down{b}"))
                        fs = range(3 * later, 3 * later + 3)
                        product(pB[b][:, (t % 2) * D:(t % 2 + 1) * D],
                                [(gu[0:FW[f], f, t * P:(t + 1) * P], w_fd_s[0:FW[f], f, :]) for f in fs], fs, FB, p_ready[b] if n % 4 == 3 else None)
                    if k in at["pe_xlT"]:
                        j = at["pe_xlT"].index(k)
                        pe.wait_ge(s["row_ready"], c + 1)
                        pe.wait_ge(s["a_free"], before(A_RING, i, f"xlT{j}"))
                        transposes(aB, [row[:, t, j * P:(j + 1) * P] for t in range(NT)], s["a_ready"])
                    if k == at["pe_logits"]:
                        pe.wait_ge(s["a_free"], before(A_RING, i, "logits"))
                        for t in range(NT):
                            product(aB[:, t * NE:(t + 1) * NE], [(xlT[:, j, t * P:(t + 1) * P], wg_s[:, j, :]) for j in range(KD)],
                                    range(KD), KD, s["a_ready"] if t == NT - 1 else None)
                    if k == at["pe_counts"]:
                        if first(c, 0):
                            pe.wait_ge(s["tables_ready"], 1)
                        pe.wait_ge(s["a_free"], before(A_RING, i, "counts"))
                        pe.wait_ge(s["oh_ready"], 5 * c + 1)
                        for t in range(NT):
                            product(aB[:, t * NE:(t + 1) * NE],
                                    [(ones_b[:, :], ohb[:, j, :]) for j in range(t)] + [(earlier_b[:, :], ohb[:, t, :])], range(t + 1), t + 1)
                        product(aB[:, NT * NE:NT * NE + NE], [(ones_b[:, :], ohb[:, j, :]) for j in range(NT)], range(NT), NT, s["a_ready"])

                iterations(pe, iteration)

        with ExitStack() as ctx:
            def sb(name, shape, dt=F32):
                return ctx.enter_context(nc.sbuf_tensor(name, shape, dt))

            def bank(name):
                return ctx.enter_context(nc.psum_tensor(name, [P, 512], F32))

            G = C // T
            NG = NE * G
            TURN = max(2 * G, 4)
            TURNS = NG // TURN
            w1_hi, w1_lo = ([sb(f"w1_{part}{i}", [P, KD, H], F32R) for i in range(2)] for part in ("hi", "lo"))
            w2_hi, w2_lo = ([sb(f"w2_{part}{i}", [P, HB, D], F32R) for i in range(2)] for part in ("hi", "lo"))
            xe_hi, xe_lo = ([sb(f"xe_{part}{i}", [P, KD, T], F32R) for i in range(2)] for part in ("hi", "lo"))
            h1_hi, h1_lo = ([sb(f"h1_{part}{i}", [P, HB, T], F32R) for i in range(2)] for part in ("hi", "lo"))
            h1_stage = sb("h1_stage", [P, 4, T])
            b1_s = [sb(f"b1_{i}", [P, HB]) for i in range(2)]
            b2_s = [sb(f"b2_{i}", [P, D]) for i in range(2)]
            rows = [sb(f"rows{i}", [P, NT, ROW]) for i in range(TURN)]
            y = [sb(f"y{i}", [P, NT, D]) for i in range(2)]
            st2 = sb("st2", [P, NT, 6])
            mv2 = sb("mv2", [P, NT, 2])
            lv2, y02, vv2, tt2, rs2 = (sb(f"{n}2", [P, NT]) for n in ("lv", "y0", "vv", "tt", "rs"))
            x_bank = [bank(f"x_bank{i}") for i in range(2)]
            h_bank = [bank(f"h_bank{i}") for i in range(4)]
            o_bank = [bank(f"o_bank{i}") for i in range(2)]
            s = {n: ctx.enter_context(nc.semaphore(n)) for n in """w1_high w2_high w1_low w2_low
                xt_ready xt_high xt_low hid_ready hid_free hid_low o_ready o_free y_ready y_stats y_aggr y_ln y_y0 y_newton y_rs yn_ready""".split()}
            bias_loaded = [ctx.enter_context(nc.semaphore(f"bias_loaded{i}")) for i in range(2)]
            rows_loaded = [ctx.enter_context(nc.semaphore(f"rows_loaded{i}")) for i in range(TURN)]
            passed_sp, passed_pool, passed_dve = (ctx.enter_context(nc.semaphore(f"passed2_{e}")) for e in ("sp", "pool", "dve"))
            out_stored = [ctx.enter_context(nc.semaphore(f"out_stored{i}")) for i in range(TURN)]
            assert NG % TURN == 0 and TURN % (2 * G) == 0 and TURNS >= 2
            block = ctx.enter_context(nc.Block())

            def groups(eng, one):
                def turn(k):
                    for j in range(TURN):
                        one(k * (TURN // G) + j // G, k * TURN + j, j, k)

                turn(0)
                if TURNS > 2:
                    with eng.Fori(1, TURNS - 1) as k:
                        turn(k)
                turn(TURNS - 1)

            def buffer_of(j):
                return j % TURN // G % 2

            def fills(j, k):
                return k * (TURN // G // 2) + (j // G // 2 + 1)

            @block.sync
            def _(sp):
                def one(e, g, j, k):
                    if j % G == 0 and not first(e, 0):
                        sp.wait_ge(s["w1_low"], KD * e)
                        sp.sem_inc(passed_sp, 1)
                        load_w1(sp, e)
                        sp.wait_ge(s["w2_low"], e)
                        sp.sem_inc(passed_sp, 1)
                        load_w2(sp, e)
                    if some(v := k * (16 * NT)):
                        sp.wait_ge(out_stored[j], v)
                        sp.sem_inc(passed_sp, 1)
                    sp.dma_start(rows[j][:, :, :], chunk_rows(slots_dram, g)).then_inc(rows_loaded[j], 16)
                    if j % G == G - 1:
                        if some(v := e * (2 * G) - 2 * G):
                            sp.wait_ge(s["o_free"], v)
                            sp.sem_inc(passed_sp, 1)
                        for dst, src in ((b1_s[buffer_of(j)][:, :], b1[bass.ds(e, 1), :, :].rearrange("o p k -> p (o k)")),
                                         (b2_s[buffer_of(j)][:, :], b2[bass.ds(e, 1), :].rearrange("o d -> (o d)").partition_broadcast(P))):
                            sp.dma_start(dst, src).then_inc(bias_loaded[buffer_of(j)], 16)

                groups(sp, one)
                for j in range(TURN):
                    sp.wait_ge(out_stored[j], TURNS * 16 * NT)

            @block.tensor
            def _(pe):
                def turn_rows(g, j, k):
                    pe.wait_ge(rows_loaded[j], k * 16 + 16)
                    for kd in range(KD):
                        if some(v := 2 * g + kd - 1):
                            pe.wait_ge(s["xt_low"], v)
                        for t in range(NT):
                            last = pe.matmul(x_bank[kd][:, t * P:(t + 1) * P], rows[j][:, t, kd * P:(kd + 1) * P], ident,
                                             start=True, stop=True, is_transpose=True)
                        last.then_inc(s["xt_ready"], 1)

                def product(to, pairs):
                    for n, (w_hi, w_lo, v_hi, v_lo) in enumerate(pairs):
                        pe.matmul(to, w_hi, v_hi, start=(n == 0), stop=False)
                        pe.matmul(to, w_hi, v_lo, start=False, stop=False)
                        last = pe.matmul(to, w_lo, v_hi, start=False, stop=(n == len(pairs) - 1))
                    return last

                def down(e, g, j):
                    gp, ep = j % 2, buffer_of(j)
                    pe.wait_ge(s["w2_low"], e + 1)
                    pe.wait_ge(s["hid_low"], HB * g + HB)
                    for m in range(2):
                        if some(v := 2 * g + m - 1):
                            pe.wait_ge(s["o_free"], v)
                        for i in range(2):
                            t = slice((2 * m + i) * P, (2 * m + i + 1) * P)
                            last = product(o_bank[m][:, i * D:(i + 1) * D],
                                           [(h1_hi[gp][:, f, t], h1_lo[gp][:, f, t], w2_hi[ep][:, f, :], w2_lo[ep][:, f, :]) for f in range(HB)])
                        last.then_inc(s["o_ready"], 1)

                def one(e, g, j, k):
                    gp, ep = j % 2, buffer_of(j)
                    if first(g, 0):
                        turn_rows(0, 0, 0)
                    pe.wait_ge(s["w1_low"], KD * e + KD)
                    pe.wait_ge(s["xt_low"], 2 * g + 2)
                    for f in range(HB):
                        if some(v := HB * g + f - 3):
                            pe.wait_ge(s["hid_free"], v)
                        h = slice(f * P, (f + 1) * P)
                        product(h_bank[f % 4][:, :], [(w1_hi[ep][:, kd, h], w1_lo[ep][:, kd, h], xe_hi[gp][:, kd, :], xe_lo[gp][:, kd, :])
                                                      for kd in range(KD)]).then_inc(s["hid_ready"], 1)
                    if not first(g, NG - 1):
                        turn_rows(g + 1, (j + 1) % TURN, k + (j + 1) // TURN)
                    if not first(g, 0):
                        down(e - 1 if j % G == 0 else e, g - 1, j - 1)

                groups(pe, one)
                down(NE - 1, NG - 1, TURN - 1)

            @block.scalar
            def _(act):
                act.preload_act_table_set(EXP_LN)

                def norm(g):
                    act.wait_ge(s["y_aggr"], g + 1)
                    act.activation(lv2[:, :], mv2[:, :, 1], ACT.Ln, bias=eps_ln[:, 0:1]).then_inc(s["y_ln"], 1)
                    act.wait_ge(s["y_ln"], g + 1)
                    act.activation(y02[:, :], lv2[:, :], ACT.Exp, scale=-0.5).then_inc(s["y_y0"], 1)

                def split_weights(e, ep):
                    act.wait_ge(w1_loaded, e * 16 + 16)
                    if some(v := e * (2 * G) - 2 * G):
                        act.wait_ge(s["o_ready"], v)
                    for kd in range(KD):
                        act.activation(w1_hi[ep][:, kd, :], w1_stage[:, kd, :], ACT.Copy).then_inc(s["w1_high"], 1)
                    act.wait_ge(w2_loaded, e * 16 + 16)
                    act.activation(w2_hi[ep][:, :, :], w2_stage[:, :, :], ACT.Copy).then_inc(s["w2_high"], 1)

                def split_rows(g, j):
                    for kd in range(KD):
                        act.wait_ge(s["xt_ready"], 2 * g + (kd + 1))
                        act.activation(xe_hi[j % 2][:, kd, :], x_bank[kd][:, :], ACT.Copy).then_inc(s["xt_high"], 1)

                def one(e, g, j, k):
                    gp, ep = j % 2, buffer_of(j)
                    if first(g, 0):
                        split_weights(0, 0)
                        split_rows(0, 0)
                    if j % G == 0:
                        act.wait_ge(bias_loaded[ep], fills(j, k) * 32)
                    for f in range(HB):
                        act.wait_ge(s["hid_ready"], HB * g + f + 1)
                        act.activation(h1_hi[gp][:, f, :], h_bank[f % 4][:, :], ACT.Relu, bias=b1_s[ep][:, f:f + 1])
                        if some(v := HB * g + f - 3):
                            act.wait_ge(s["hid_low"], v)
                        act.activation(h1_stage[:, f % 4, :], h_bank[f % 4][:, :], ACT.Relu, bias=b1_s[ep][:, f:f + 1]).then_inc(s["hid_free"], 1)
                        if f == 5 and (not isinstance(g, int) or g > 1):
                            norm(g - 2)
                    if not first(g, NG - 1):
                        split_rows(g + 1, j + 1)
                    if j % G == G - 1 and not first(e, NE - 1):
                        split_weights(e + 1, 1 - ep)

                groups(act, one)
                norm(NG - 2)
                norm(NG - 1)

            @block.vector
            def _(dve):
                def split_weights(e, ep):
                    for kd in range(KD):
                        dve.wait_ge(s["w1_high"], KD * e + (kd + 1))
                        dve.tensor_tensor(w1_lo[ep][:, kd, :], w1_stage[:, kd, :], w1_hi[ep][:, kd, :].bitcast(F32), ALU.subtract).then_inc(s["w1_low"], 1)

                def split_rows(g, j):
                    for kd in range(KD):
                        dve.wait_ge(s["xt_high"], 2 * g + (kd + 1))
                        dve.tensor_tensor(xe_lo[j % 2][:, kd, :], x_bank[kd][:, :], xe_hi[j % 2][:, kd, :].bitcast(F32), ALU.subtract).then_inc(s["xt_low"], 1)

                def bias_and_gate(g, j, k):
                    j %= TURN
                    gp, ep = j % 2, buffer_of(j)
                    dve.wait_ge(bias_loaded[ep], fills(j, k) * 32)
                    if some(v := k * (16 * NT) + (16 * NT if j >= 2 else 0)):
                        dve.wait_ge(out_stored[(j - 2) % TURN], v)
                    for m in range(2):
                        dve.wait_ge(s["o_ready"], 2 * g + (m + 1))
                        dve.tensor_tensor(y[gp][:, 2 * m:2 * m + 2, :], o_bank[m][:, :].rearrange("p (t d) -> p t d", d=D),
                                          b2_s[ep][:, :].unsqueeze(1).broadcast_to([P, 2, D]), ALU.add).then_inc(s["o_free"], 1)
                    dve.wait_ge(s["o_free"], 2 * g + 2)
                    for t in range(NT):
                        last = dve.scalar_tensor_tensor(out=y[gp][:, t, :], in0=y[gp][:, t, :], scalar=rows[j][:, t, D:D + 1],
                                                        in1=rows[j][:, t, 0:D], op0=ALU.mult, op1=ALU.add)
                    last.then_inc(s["y_ready"], 1)
                    dve.wait_ge(s["y_ready"], g + 1)
                    for t in range(NT):
                        last = dve.bn_stats(st2[:, t, :], y[gp][:, t, :])
                    last.then_inc(s["y_stats"], 1)
                    dve.wait_ge(s["y_stats"], g + 1)
                    dve.sem_inc(passed_dve, 1)
                    for t in range(NT):
                        last = dve.bn_aggr(mv2[:, t, :], st2[:, t, :])
                    last.then_inc(s["y_aggr"], 1)

                def normalize(g, gp):
                    dve.wait_ge(s["y_y0"], g + 1)
                    dve.tensor_scalar(vv2[:, :], mv2[:, :, 1], 1.0, LN_EPS, ALU.mult, ALU.add)
                    dve.tensor_tensor(tt2[:, :], y02[:, :], y02[:, :], ALU.mult).then_inc(s["y_newton"], 1)
                    dve.wait_ge(s["y_newton"], 3 * g + 1)
                    dve.tensor_tensor(tt2[:, :], tt2[:, :], vv2[:, :], ALU.mult).then_inc(s["y_newton"], 1)
                    dve.wait_ge(s["y_newton"], 3 * g + 2)
                    dve.tensor_scalar(tt2[:, :], tt2[:, :], -0.5, 1.5, ALU.mult, ALU.add).then_inc(s["y_newton"], 1)
                    dve.wait_ge(s["y_newton"], 3 * g + 3)
                    dve.tensor_tensor(rs2[:, :], y02[:, :], tt2[:, :], ALU.mult).then_inc(s["y_rs"], 1)
                    dve.wait_ge(s["y_rs"], g + 1)
                    for t in range(NT):
                        last = dve.tensor_scalar(y[gp][:, t, :], y[gp][:, t, :], mv2[:, t, 0:1], rs2[:, t:t + 1], ALU.subtract, ALU.mult)
                    last.then_inc(s["yn_ready"], 1)

                def one(e, g, j, k):
                    gp, ep = j % 2, buffer_of(j)
                    if first(g, 0):
                        split_weights(0, 0)
                        split_rows(0, 0)
                    for f in range(HB):
                        dve.wait_ge(s["hid_free"], HB * g + f + 1)
                        dve.tensor_tensor(h1_lo[gp][:, f, :], h1_stage[:, f % 4, :], h1_hi[gp][:, f, :].bitcast(F32), ALU.subtract).then_inc(s["hid_low"], 1)
                        if f == 6 and (not isinstance(g, int) or g > 1):
                            normalize(g - 2, gp)
                    if not first(g, NG - 1):
                        split_rows(g + 1, j + 1)
                    if j % G == G - 1 and not first(e, NE - 1):
                        split_weights(e + 1, 1 - ep)
                    if not first(g, 0):
                        bias_and_gate(g - 1, j - 1, k if j > 0 else k - 1)

                groups(dve, one)
                normalize(NG - 2, (NG - 2) % 2)
                bias_and_gate(NG - 1, TURN - 1, TURNS - 1)
                normalize(NG - 1, (NG - 1) % 2)

            @block.gpsimd
            def _(pool):
                def split_weights(e, ep):
                    pool.wait_ge(s["w2_high"], e + 1)
                    pool.tensor_tensor(w2_lo[ep][:, :, :], w2_stage[:, :, :], w2_hi[ep][:, :, :].bitcast(F32), ALU.subtract).then_inc(s["w2_low"], 1)

                def scatter(g, j):
                    pool.wait_ge(s["yn_ready"], g + 1)
                    pool.sem_inc(passed_pool, 1)
                    for t in range(NT):
                        pool.indirect_dma_start(out=out_rows, out_offset=bass.IndirectOffsetOnAxis(rows[j][:, :, :].bitcast(U32)[:, t, D + 1:D + 2], 0),
                                                in_=y[j % 2][:, t, :], in_offset=None, bounds_check=S - 1,
                                                oob_is_err=False).then_inc(out_stored[j], 16)

                def one(e, g, j, k):
                    if first(g, 0):
                        split_weights(0, 0)
                    if not isinstance(g, int) or g > 1:
                        scatter(g - 2, (j - 2) % TURN)
                    if j % G == G - 1 and not first(e, NE - 1):
                        split_weights(e + 1, 1 - buffer_of(j))

                groups(pool, one)
                scatter(NG - 2, TURN - 2)
                scatter(NG - 1, TURN - 1)

    return nc


def kernel(**inputs):
    import numpy as np
    import concourse.bacc as bacc
    from concourse.bass_utils import run_bass_kernel_spmd

    a = {k.replace("L0_attn_", "").replace("L0_ffn_", "moe_"): np.asarray(v) for k, v in inputs.items()}
    B, L, D = a["x"].shape
    NE, _, H = a["moe_w1"].shape
    DI, NS = a["A_log"].shape
    S = B * L
    NCH = S // T
    columns, n_consts = constants_layout(D, NE, NCH)

    consts = np.zeros((P, n_consts), np.float32)
    for name, table in (
        ("ident", np.eye(P)),
        ("earlier", np.triu(np.ones((P, P)), 1)),
        ("ones", np.ones((P, P))),
        ("rank", NE - np.arange(NE)[None]),
        ("base", (S // NE) * np.arange(NE)[None]),
        ("keep", (np.arange(NCH + 1) % (L // T) != 0)[None]),
        ("token", np.arange(P)[:, None] + P * np.arange(NT)[None]),
    ):
        consts[:, columns[name][0]:columns[name][1]] = table

    def by_partition(v):
        return v.reshape(-1, P).T

    arrays = dict(
        x=a["x"], norm1=by_partition(a["norm1_w"]), w_in=a["in_proj_w"].T, w_gate=a["gate_proj_w"].T, w_dt=a["dt_w"].T,
        dt_b=by_partition(a["dt_b"]), w_x=a["x_proj_w"].T, a_log=a["A_log"].reshape(DI // P, P, NS).transpose(1, 0, 2),
        dp=by_partition(a["Dp"]), w_out=a["out_proj_w"].T, norm2=by_partition(a["ffn_norm_w"]),
        w_fg=a["ffn_gate_w"].T, w_fu=a["ffn_up_w"].T, w_fd=a["ffn_down_w"].T,
        wg=a["moe_wg"], w1=a["moe_w1"], b1=a["moe_b1"].reshape(NE, H // P, P).transpose(0, 2, 1), w2=a["moe_w2"], b2=a["moe_b2"],
        consts=consts,
    )
    nc = bacc.Bacc("TRN2", target_bir_lowering=False, num_devices=1)
    feeds, args = {}, []
    for name, v in arrays.items():
        v = np.ascontiguousarray(v)
        feeds[f"in_{name}"] = v
        args.append(nc.dram_tensor(f"in_{name}", v.shape, mybir.dt.from_np(v.dtype), kind="ExternalInput").ap())
    args.append(nc.dram_tensor("out_0", (B, L, D), F32, kind="ExternalOutput").ap())
    build(nc, *args)
    r = run_bass_kernel_spmd(nc, [feeds], core_ids=[0])
    return r.results[0]["out_0"]
```
